# Optimizing a Trainium2 kernel written in Bass

```python
import numpy as np
import jax
import jax.numpy as jnp

def _softmax(x, axis=-1):
    return jax.nn.softmax(x, axis=axis)

def _gelu(x):
    return jax.nn.gelu(x, approximate=True)

def _silu(x):
    return jax.nn.silu(x)

def _sigmoid(x):
    return jax.nn.sigmoid(x)

def _layernorm(x, axis=-1, eps=1e-05):
    m = jnp.mean(x, axis=axis, keepdims=True)
    v = jnp.var(x, axis=axis, keepdims=True)
    return (x - m) / jnp.sqrt(v + eps)

def _scatter_add(tgt, idx, src, axis=0):
    return tgt.at[idx].add(src)

def _segment_sum(src, seg, n):
    return jax.ops.segment_sum(src, seg, n)
kernel_name = 'mk_adj_preln_d2_adj_r2_6ce142'

def setup_inputs(seed: int=0):
    np.random.seed(seed)
    _w = jnp.asarray

    def _rec_inputs():
        import jax
        import jax.numpy as jnp
        _gk = jax.random.key(seed)
        x = -0.0002928 + 1 * jax.random.normal(jax.random.fold_in(_gk, 1), (4096, 256), jnp.float32)
        _w = (1.0 + jnp.arange(4096, dtype=jnp.float32)) ** (-0.5)
        _w = _w / _w.mean()
        _pij = jnp.clip(0.000488281 * _w[:, None] * _w[None, :], 0.0, 1.0)
        _a = jax.random.uniform(jax.random.fold_in(_gk, 2), (4096, 4096)) < _pij
        _af = _a.astype(jnp.float32)
        adj = _af
        return (x, adj)
    x, adj = _rec_inputs()

    def _L0_gnn_setup():
        import jax, jax.numpy as jnp
        import numpy as np
        N = 4096
        D_IN = 256
        HEADS = 8
        DPH = 256 // HEADS
        EDGE_P = 0.01
        key = jax.random.key(seed)
        k1, k2, k3 = jax.random.split(key, 3)
        H = jax.random.normal(k1, (N, D_IN), dtype=jnp.float32)
        adj = (jax.random.uniform(k2, (N, N)) < EDGE_P).astype(jnp.float32)
        limit = float(np.sqrt(6.0 / (D_IN + DPH)))
        W = jax.random.uniform(k3, (HEADS, D_IN, DPH), jnp.float32, -limit, limit)
        b = jnp.zeros((HEADS, DPH), jnp.float32)
        return {'H': H, 'adj': adj, 'W': W, 'b': b}
    _L0_gnn_all = _L0_gnn_setup()
    _L0_gnn_in = {k: v for k, v in _L0_gnn_all.items() if k in ('W', 'b')}
    del _L0_gnn_all

    def _L1_gnn_setup():
        import jax, jax.numpy as jnp
        import numpy as np
        N = 4096
        DIN = 256
        DOUT = 256
        key = jax.random.key(seed)
        k1, k2, k3 = jax.random.split(key, 3)
        H_in = jax.random.normal(k1, (N, DIN), dtype=jnp.float32)
        u = jax.random.uniform(k2, (N, N), dtype=jnp.float32)
        upper = (u < 0.005).astype(jnp.float32)
        upper = jnp.triu(upper, k=1)
        A = upper + upper.T
        limit = np.sqrt(6.0 / (DIN + DOUT)).astype(np.float32)
        W = jax.random.uniform(k3, (DIN, DOUT), dtype=jnp.float32, minval=-limit, maxval=limit)
        return {'H_in': H_in, 'A': A, 'W': W}
    _L1_gnn_all = _L1_gnn_setup()
    _L1_gnn_in = {k: v for k, v in _L1_gnn_all.items() if k in ('W',)}
    del _L1_gnn_all
    return {'x': x, 'adj': adj, 'L0_gnn_W': _L0_gnn_in['W'], 'L0_gnn_b': _L0_gnn_in['b'], 'L1_gnn_W': _L1_gnn_in['W']}

def reference(x, adj, L0_gnn_W, L0_gnn_b, L1_gnn_W):
    import jax
    import jax.numpy as jnp

    def _L0_gnn_ref(H, adj, W, b):
        import jax, jax.numpy as jnp
        import numpy as np
        N = 4096
        D_IN = 256
        HEADS = 8
        DPH = 256 // HEADS
        EDGE_P = 0.01
        H_ = jnp.einsum('nd,hde->hne', H, W)
        out = jnp.einsum('nm,hme->hne', adj, H_) + b[:, None, :]
        return jnp.transpose(out, (1, 0, 2)).reshape(H.shape[0], HEADS * DPH)

    def _L1_gnn_ref(H_in, A, W):
        import jax, jax.numpy as jnp
        import numpy as np
        N = 4096
        DIN = 256
        DOUT = 256
        A_ = A + jnp.eye(A.shape[0], dtype=A.dtype)
        d_inv_sqrt = jax.lax.rsqrt(A_.sum(axis=1))
        A_norm = A_ * d_inv_sqrt[:, None] * d_inv_sqrt[None, :]
        H_out = jnp.matmul(jnp.matmul(A_norm, H_in), W)
        return jax.nn.relu(H_out)
    h = jnp.maximum(_layernorm(x, axis=-1), 0.0)
    x = x + _L0_gnn_ref(h, adj, L0_gnn_W, L0_gnn_b)
    h = jnp.maximum(_layernorm(x, axis=-1), 0.0)
    x = x + _L1_gnn_ref(h, adj, L1_gnn_W)
    return x

_drawn_inputs = setup_inputs


def setup_inputs(seed=0):
    import zlib

    import numpy as np

    out = dict(_drawn_inputs(seed))
    spreads = {'L0_gnn_b': (0.0, 0.1)}
    factors = {}
    for name, (base, spread) in spreads.items():
        noise = np.random.default_rng([zlib.crc32(name.encode()), seed]).standard_normal(out[name].shape)
        drawn = base * np.exp(spread * noise) if base else spread * noise
        out[name] = jnp.asarray(drawn.astype(out[name].dtype))
    for name, factor in factors.items():
        out[name] = (out[name] * factor).astype(out[name].dtype)
    return out
```

```python
from contextlib import ExitStack

import concourse.bass as bass
from concourse import mybir
from concourse.alu_op_type import AluOpType as ALU

DT = mybir.dt
ACT = mybir.ActivationFunctionType

P = 128
N = 4096
D = 256
BLOCKS = N // P
CHUNK = 512
CHUNKS = N // CHUNK
BATCH = CHUNK // P
GROUP_BLOCKS = 2
GROUP = GROUP_BLOCKS * CHUNK
GROUPS = BLOCKS // GROUP_BLOCKS
STAGES = 4
RING = 8
KEPT_FIRST, KEPT_LAST = 1, CHUNKS - 2
KEPT = KEPT_LAST - KEPT_FIRST + 1
ALL0 = CHUNKS * GROUPS
CHECKS0 = KEPT * GROUPS
H_SCALE = 2.0 ** 11
A_UNIT = 2.0 ** -14
S_UNSCALE = 1.0 / (H_SCALE * A_UNIT)
EPS = 1e-5
BYTE_UNIT = 4.0
STEPS0 = (BATCH + 5) + 6 + 1


def ring_use(layer, c, g):
    return (2 * layer + (c != 0)) * GROUPS + g


def load_index(layer, c, g):
    if layer == 0:
        return c * GROUPS + g
    return ALL0 + (c != 0) * GROUPS + g


class Chain:

    def __init__(self, engine, sem):
        self.engine, self.sem, self.base, self.count = engine, sem, 0, 0

    def step(self, instruction):
        instruction.then_inc(self.sem, 1)
        self.count += 1

    def settle(self):
        self.engine.wait_ge(self.sem, self.base + self.count)

    def link(self, instruction):
        self.step(instruction)
        self.settle()


def build(nc, x_in, adj_in, w0_in, w1_in, b_in, out):
    with ExitStack() as ctx:
        def sb(name, shape, dt):
            return ctx.enter_context(nc.sbuf_tensor(name, shape, dt))

        def sem(name):
            return ctx.enter_context(nc.semaphore(name))

        kept = sb("kept", [P, KEPT * GROUPS * GROUP], DT.float8e5)
        ring = sb("ring", [P, RING * GROUP], DT.float8e5)
        stage = sb("stage", [P, STAGES, GROUP], DT.float32)
        hsplit = sb("hsplit", [P, BLOCKS, 2, D], DT.float16)
        xs = sb("xs", [P, BLOCKS, D], DT.float32)
        w = sb("w", [P, 2, D], DT.float32)
        st = sb("st", [P, 2, CHUNK], DT.float32)
        bias = sb("bias", [P, D], DT.float32)
        hfull = sb("hfull", [P, 2, BATCH, D], DT.float32)
        bad_out = sb("bad_out", [P, GROUP], DT.uint8)
        bad = sb("bad", [P, ALL0], DT.float32)
        byte_sum = sb("byte_sum", [P, GROUP // 2], DT.uint16)
        edge_sum = sb("edge_sum", [P, CHUNK], DT.bfloat16)
        per_edge = sb("per_edge", [P, 1], DT.bfloat16)
        eye = sb("eye", [P, P], DT.float32)
        eye8 = sb("eye8", [P, P], DT.float8e5)
        bn = sb("bn", [P, BATCH, 6], DT.float32)
        mean_twice = sb("mean_twice", [P, 2, BATCH], DT.float32)
        mean_diff = sb("mean_diff", [P, BATCH], DT.float32)
        m2_sum = sb("m2_sum", [P, BATCH], DT.float32)
        radicand = sb("radicand", [P, 2, CHUNKS, 2 * BATCH], DT.float32)
        root = sb("root", [P, 2, CHUNKS, 2 * BATCH], DT.float32)
        inv = sb("inv", [P, 2, CHUNKS, 2 * BATCH], DT.float32)
        newton = sb("newton", [P, 2 * BATCH], DT.float32)
        norm_scale = sb("norm_scale", [P, 2, BLOCKS], DT.float32)
        norm_bias = sb("norm_bias", [P, 2, BLOCKS], DT.float32)

        ps_s = [[ctx.enter_context(nc.psum_tensor(f"ps_s{a}{q}", [P, CHUNK], DT.float32)) for q in range(2)]
                for a in range(2)]
        ps_w = [ctx.enter_context(nc.psum_tensor(f"ps_w{j}", [P, CHUNK], DT.float32)) for j in range(BATCH)]
        ps_deg = ps_w[0][:, D:D + BATCH]

        kept16 = kept[:].bitcast(DT.uint16)
        kept32 = kept[:].bitcast(DT.uint32)
        ring16 = ring[:].bitcast(DT.uint16)
        ring32 = ring[:].bitcast(DT.uint32)
        eye32 = eye8[:].bitcast(DT.uint32)

        x_loaded = [sem(f"x_loaded{b}") for b in range(CHUNKS)]
        staged = [sem(f"staged{s}") for s in range(STAGES)]
        w_loaded = sem("w_loaded")
        bias_loaded = sem("bias_loaded")
        cast_done = sem("cast_done")
        check_done = sem("check_done")
        deg_added = sem("deg_added")
        edge_sums = sem("edge_sums")
        pe_groups = sem("pe_groups")
        s_evacuated = sem("s_evacuated")
        w_product = sem("w_product")
        w_read = sem("w_read")
        degrees_read = sem("degrees_read")
        radicand_ready = sem("radicand_ready")
        root_ready = sem("root_ready")
        norm_ready = sem("norm_ready")
        h_ready = sem("h_ready")
        split_ready = sem("split_ready")
        biased = sem("biased")
        consts = sem("consts")
        diag_added = sem("diag_added")
        out_ready = sem("out_ready")
        stored = sem("stored")
        dve_step = sem("dve_step")

        block = ctx.enter_context(nc.Block())

        def tile8(c, g):
            if KEPT_FIRST <= c <= KEPT_LAST:
                o = ((c - KEPT_FIRST) * GROUPS + g) * GROUP
                return kept[:, o:o + GROUP]
            s = g % RING
            return ring[:, s * GROUP:(s + 1) * GROUP]

        @block.sync
        def _(sp):
            def load(c, g, casts, checks=None):
                s = g % STAGES
                if casts is not None:
                    sp.wait_ge(cast_done, casts)
                if checks is not None:
                    sp.nop(nofuse=True)
                    sp.wait_ge(check_done, checks)
                src = adj_in[c, :, g * GROUP:(g + 1) * GROUP] if isinstance(c, int) else \
                    adj_in[bass.ds(c, 1), :, g * GROUP:(g + 1) * GROUP].rearrange("a p f -> (a p) f")
                sp.dma_start(stage[:, s, :], src).then_inc(staged[s], 16)

            def load_x(b):
                sp.dma_start(xs[:, b * BATCH:(b + 1) * BATCH, :],
                             x_in[:, b * BATCH * D:(b + 1) * BATCH * D].rearrange("p (j d) -> p j d", d=D)
                             ).then_inc(x_loaded[b], 16)

            load_x(0)
            for g in range(GROUPS):
                load(0, g, g - STAGES + 1 if g >= STAGES else None)
                if g % 2 == 0 and g // 2 + 1 < CHUNKS:
                    load_x(g // 2 + 1)
                if g == 1:
                    sp.dma_start(bias[:], b_in.partition_broadcast(P)).then_inc(bias_loaded, 16)
                if g == 7:
                    sp.dma_start(w[:], w0_in.rearrange("(q p) e -> p q e", p=P)).then_inc(w_loaded, 16)
            for g in range(GROUPS):
                load(1, g, GROUPS + g - STAGES + 1, g - STAGES + 1 if g >= STAGES else None)
            with sp.Fori(2, KEPT_LAST + 1) as c:
                for g in range(GROUPS):
                    load(c, g, c * GROUPS + (g - STAGES + 1), (c - 1) * GROUPS + (g - STAGES + 1))
            for g in range(GROUPS):
                load(CHUNKS - 1, g, (CHUNKS - 1) * GROUPS + g - STAGES + 1, min(CHECKS0, CHECKS0 + g - STAGES + 1))
            for i, c in enumerate((0, CHUNKS - 1)):
                for g in range(GROUPS):
                    load(c, g, ALL0 + i * GROUPS + g - STAGES + 1, max(CHECKS0, CHECKS0 + i * GROUPS + g - STAGES + 1))
                    if c == 0 and g == 8:
                        sp.wait_ge(w_product, CHUNKS * BATCH)
                        sp.dma_start(w[:], w1_in.rearrange("(q p) e -> p q e", p=P)).then_inc(w_loaded, 16)

        @block.tensor
        def _(pe):
            def w_products(layer, c):
                pe.wait_ge(s_evacuated, layer * (2 * CHUNKS) + 2 * (c + 1))
                pe.wait_ge(w_loaded, layer * 16 + 16)
                for j in range(BATCH):
                    if c > 0:
                        pe.wait_ge(w_read, layer * (CHUNKS * BATCH) + ((c - 1) * BATCH + j + 1))
                    if j == 0 and c > 0:
                        pe.wait_ge(degrees_read, c)
                    if j == 0:
                        with pe.If(layer == 0):
                            pe.wait_ge(edge_sums, c + 1)
                            for i in range(BATCH):
                                nc.tensor.matmul(ps_deg[:, i:i + 1], edge_sum[:, i * P:(i + 1) * P], per_edge[:],
                                                 start=True, stop=True)
                    for q in range(2):
                        last = nc.tensor.matmul(ps_w[j][:, 0:D], st[:, q, j * P:(j + 1) * P], w[:, q, :],
                                                start=q == 0, stop=q == 1)
                    last.then_inc(w_product, 1)

            if True:
                pe.wait_ge(consts, 3)
                with pe.Fori(0, 2) as layer:
                    for c in range(CHUNKS):
                        for g in range(GROUPS):
                            if c == 0 and g % 2 == 0:
                                pe.wait_ge(split_ready, layer * CHUNKS + (g // 2 + 1))
                            if g // 2 == c:
                                pe.wait_ge(diag_added, layer * (c + 1) + 1)
                            pe.wait_ge(cast_done, c * GROUPS + g + 1)
                            if not KEPT_FIRST <= c <= KEPT_LAST:
                                again = ALL0 - (c != 0) * KEPT * GROUPS
                                pe.wait_ge(cast_done, layer * again + (c * GROUPS + g + 1))
                            pe.nop(nofuse=True)
                            for i in range(GROUP_BLOCKS):
                                m = g * GROUP_BLOCKS + i
                                for q in range(2):
                                    for part in range(2):
                                        last = nc.tensor.matmul(
                                            ps_s[c % 2][q][:], hsplit[:, m, part, q * P:(q + 1) * P],
                                            tile8(c, g)[:, i * CHUNK:(i + 1) * CHUNK],
                                            start=m == 0 and part == 0, stop=m == BLOCKS - 1 and part == 1)
                            last.then_inc(pe_groups, 1)
                            if c > 0 and g == 1:
                                w_products(layer, c - 1)
                    w_products(layer, CHUNKS - 1)

        @block.scalar
        def _(act):
            act.wait_ge(consts, 2)
            act.activation(eye8[:], eye[:], ACT.Copy, scale=A_UNIT, saturate=False).then_inc(diag_added, 1)

            def cast(layer, c, g):
                n = load_index(layer, c, g)
                act.wait_ge(staged[n % STAGES], 16 * (n // STAGES + 1))
                if not KEPT_FIRST <= c <= KEPT_LAST:
                    u = ring_use(layer, c, g) - RING
                    if u >= 0:
                        ulayer, rest = divmod(u, 2 * GROUPS)
                        uc, ug = (CHUNKS - 1) * (rest // GROUPS), rest % GROUPS
                        act.wait_ge(pe_groups, (ulayer * CHUNKS + uc) * GROUPS + ug + 1)
                        act.wait_ge(deg_added, min(ALL0, (ulayer * CHUNKS + uc) * GROUPS + ug + 1))
                nc.scalar.activation(tile8(c, g), stage[:, n % STAGES, :], ACT.Copy, scale=A_UNIT,
                                     saturate=False).then_inc(cast_done, 1)

            def square_roots(layer, b):
                k = 4 if layer == 0 else 8
                act.wait_ge(radicand_ready, layer * CHUNKS + b + 1)
                nc.scalar.activation(root[:, layer, b, 0:k], radicand[:, layer, b, 0:k], ACT.Sqrt
                                     ).then_inc(root_ready, 1)

            def normalise(layer, b):
                act.wait_ge(norm_ready, layer * CHUNKS + b + 1)
                if layer * CHUNKS + b >= 2:
                    act.wait_ge(split_ready, layer * CHUNKS + b - 1)
                for j in range(BATCH):
                    m = b * BATCH + j
                    last = nc.scalar.activation(hfull[:, b % 2, j, :], xs[:, m, :], ACT.Relu,
                                                bias=norm_bias[:, layer, m:m + 1], scale=norm_scale[:, layer, m:m + 1])
                last.then_inc(h_ready, 1)

            def evacuate(layer, c):
                k = layer * CHUNKS + c
                act.wait_ge(pe_groups, (k + 1) * GROUPS)
                if k > 0:
                    act.wait_ge(w_product, BATCH * k)
                for q in range(2):
                    nc.scalar.activation(st[:, q, :], ps_s[c % 2][q][:], ACT.Copy, scale=S_UNSCALE
                                         ).then_inc(s_evacuated, 1)

            square_roots(0, 0)
            for b in range(CHUNKS):
                cast(0, 0, 2 * b)
                if b + 1 < CHUNKS:
                    square_roots(0, b + 1)
                normalise(0, b)
                cast(0, 0, 2 * b + 1)
            for c in range(1, CHUNKS - 1):
                for g in range(GROUPS):
                    cast(0, c, g)
                    if g == 7:
                        evacuate(0, c - 1)
                    if g == 13:
                        square_roots(1, c - 1)
            for g in range(GROUPS):
                cast(0, CHUNKS - 1, g)
                if g == 7:
                    evacuate(0, CHUNKS - 2)
                if g == 9:
                    square_roots(1, CHUNKS - 2)
                if g in (10, 12, 14):
                    normalise(1, (g - 10) // 2)
            for g in range(RING):
                cast(1, 0, g)
                if g % 2 == 0:
                    normalise(1, 3 + g // 2)
            evacuate(0, CHUNKS - 1)
            square_roots(1, CHUNKS - 1)
            normalise(1, CHUNKS - 1)
            for g in range(RING, GROUPS):
                cast(1, 0, g)
            for g in range(RING):
                cast(1, CHUNKS - 1, g)
            for c in range(CHUNKS - 1):
                evacuate(1, c)
            for g in range(RING, GROUPS):
                cast(1, CHUNKS - 1, g)
            evacuate(1, CHUNKS - 1)

        @block.vector
        def _(dve):
            chain = Chain(dve, dve_step)

            def statistics(layer, b):
                turn = b % 2 if layer == 0 else 0
                if layer == 0 and b > 0:
                    dve.wait_ge(radicand_ready, b)
                if layer == 0 and b > 1:
                    dve.wait_ge(norm_ready, b - 1)
                for j in range(BATCH):
                    chain.step(nc.vector.bn_stats(bn[:, j, :], block_of(xs, b * BATCH + j)))
                mean_even, m2_even, mean_odd, m2_odd = (bn[:, :, i] for i in (1, 2, 4, 5))
                chain.settle()
                chain.step(nc.vector.tensor_tensor(mean_twice[:, turn], mean_even, mean_odd, ALU.add))
                chain.step(nc.vector.tensor_tensor(mean_diff[:], mean_even, mean_odd, ALU.subtract))
                chain.step(nc.vector.tensor_tensor(m2_sum[:], m2_even, m2_odd, ALU.add))
                chain.settle()
                chain.step(nc.vector.scalar_tensor_tensor(out=mean_diff[:], in0=mean_diff[:], scalar=0.25,
                                                          in1=mean_diff[:], op0=ALU.mult, op1=ALU.mult))
                chain.step(nc.vector.tensor_scalar(m2_sum[:], m2_sum[:], 1.0 / D, EPS, ALU.mult, ALU.add))
                chain.settle()
                nc.vector.tensor_tensor(part_of(radicand, layer, b, 0, BATCH), m2_sum[:], mean_diff[:], ALU.add
                                        ).then_inc(radicand_ready, 1)

            def block_of(t, m):
                return t[:, m, :] if isinstance(m, int) else t[:, bass.ds(m, 1), :].rearrange("p a d -> p (a d)")

            def part_of(t, layer, b, lo, hi):
                v = t[:, layer]
                return v[:, b, lo:hi] if isinstance(b, int) else \
                    v[:, bass.ds(b, 1), lo:hi].rearrange("p a d -> p (a d)")

            def four_of(t, layer, b):
                v = t[:, layer, :]
                return v[:, b * BATCH:(b + 1) * BATCH] if isinstance(b, int) else v[:, bass.ds(b * BATCH, BATCH)]

            def scales(layer, b):
                k = BATCH * (layer + 1)
                rad, iv = part_of(radicand, layer, b, 0, k), part_of(inv, layer, b, 0, k)
                nw = newton[:, 0:k]
                dve.wait_ge(root_ready, b + (layer * CHUNKS + 1))
                chain.link(nc.vector.reciprocal(iv, part_of(root, layer, b, 0, k)))
                chain.link(nc.vector.tensor_tensor(nw, iv, iv, ALU.mult))
                chain.link(nc.vector.tensor_tensor(nw, nw, rad, ALU.mult))
                chain.link(nc.vector.tensor_scalar(nw, nw, -0.5, 1.5, ALU.mult, ALU.add))
                chain.link(nc.vector.tensor_tensor(iv, iv, nw, ALU.mult))
                if layer == 0:
                    chain.link(nc.vector.tensor_scalar(four_of(norm_scale, 0, b), iv, H_SCALE, None, ALU.mult))
                else:
                    chain.link(nc.vector.scalar_tensor_tensor(
                        out=four_of(norm_scale, 1, b), in0=part_of(inv, 1, b, 0, BATCH), scalar=H_SCALE,
                        in1=part_of(inv, 1, b, BATCH, 2 * BATCH), op0=ALU.mult, op1=ALU.mult))
                nc.vector.scalar_tensor_tensor(
                    out=four_of(norm_bias, layer, b), in0=mean_twice[:, b % 2 if layer == 0 else 0], scalar=-0.5,
                    in1=four_of(norm_scale, layer, b), op0=ALU.mult, op1=ALU.mult).then_inc(norm_ready, 1)

            def split(layer, b):
                dve.wait_ge(h_ready, layer * CHUNKS + b + 1)
                if layer == 1:
                    dve.wait_ge(pe_groups, (CHUNKS - 1) * GROUPS + 2 * b + 2)
                high, low = (hsplit[:, b * BATCH:(b + 1) * BATCH, i, :] for i in range(2))
                chain.link(nc.vector.tensor_copy(high, hfull[:, b % 2]))
                nc.vector.tensor_tensor(low, hfull[:, b % 2], high, ALU.subtract).then_inc(split_ready, 1)

            def check(index, g, staged_count):
                s = g % STAGES
                dve.wait_ge(staged[s], staged_count)
                if not (isinstance(index, int) and index == 0):
                    dve.wait_ge(check_done, index)
                column = bad[:, index:index + 1] if isinstance(index, int) else bad[:, bass.ds(index, 1)]
                nc.vector.scalar_tensor_tensor(out=bad_out[:], in0=stage[:, s, :], scalar=1.0, in1=stage[:, s, :],
                                               op0=ALU.is_equal, op1=ALU.not_equal, accum_out=column
                                               ).then_inc(check_done, 1)

            def add_degrees(c, g):
                dve.wait_ge(cast_done, c * GROUPS + (g + 1))
                words = GROUP // 2
                if not isinstance(c, int):
                    tile = kept16[:, bass.ds(c * (GROUPS * words) + (g - GROUPS * KEPT_FIRST) * words, words)]
                elif KEPT_FIRST <= c <= KEPT_LAST:
                    tile = kept16[:, ((c - KEPT_FIRST) * GROUPS + g) * words:((c - KEPT_FIRST) * GROUPS + g + 1) * words]
                else:
                    tile = ring16[:, g % RING * words:(g % RING + 1) * words]
                if g == 0:
                    if not (isinstance(c, int) and c == 0):
                        dve.wait_ge(edge_sums, c)
                    nc.vector.tensor_copy(byte_sum[:], tile).then_inc(deg_added, 1)
                else:
                    dve.wait_ge(deg_added, c * GROUPS + g)
                    nc.vector.tensor_tensor(byte_sum[:], byte_sum[:], tile, ALU.add).then_inc(deg_added, 1)

            def fold_degrees(c):
                half = GROUP // 4
                dve.wait_ge(deg_added, c * GROUPS + GROUPS)
                chain.link(nc.vector.tensor_tensor(byte_sum[:, 0:half], byte_sum[:, 0:half], byte_sum[:, half:],
                                                   ALU.add))
                nc.vector.tensor_copy(edge_sum[:], byte_sum[:, 0:half].bitcast(DT.uint8)).then_inc(edge_sums, 1)

            def epilogue0(c):
                dve.wait_ge(biased, c + 1)
                for j in range(BATCH):
                    dve.wait_ge(w_product, c * BATCH + (j + 1))
                    rows = block_of(xs, c * BATCH + j)
                    nc.vector.tensor_tensor(rows, ps_w[j][:, 0:D], rows, ALU.add).then_inc(w_read, 1)
                dve.wait_ge(w_read, c * BATCH + BATCH)
                dve.wait_ge(radicand_ready, c + CHUNKS)
                dve.wait_ge(norm_ready, c + CHUNKS)
                nc.vector.tensor_scalar(part_of(radicand, 1, c, BATCH, 2 * BATCH), ps_deg, 1.0, None, ALU.add
                                        ).then_inc(degrees_read, 1)
                statistics(1, c)

            def epilogue1(c):
                if not (isinstance(c, int) and c == 0):
                    dve.wait_ge(out_ready, c)
                for j in range(BATCH):
                    dve.wait_ge(w_product, c * BATCH + (CHUNKS * BATCH + j + 1))
                    nc.vector.tensor_scalar(hfull[:, 0, j, :], ps_w[j][:, 0:D], part_of(inv, 1, c, BATCH + j, BATCH + j + 1),
                                            0.0, ALU.mult, ALU.max).then_inc(w_read, 1)
                dve.wait_ge(w_read, c * BATCH + (CHUNKS * BATCH + BATCH))
                rows = xs[:, c * BATCH:(c + 1) * BATCH, :] if isinstance(c, int) else xs[:, bass.ds(c * BATCH, BATCH), :]
                nc.vector.tensor_tensor(rows, hfull[:, 0], rows, ALU.add).then_inc(out_ready, 1)

            for b in range(CHUNKS + 2):
                if b < CHUNKS:
                    dve.wait_ge(x_loaded[b], 16)
                    statistics(0, b)
                if 1 <= b <= CHUNKS:
                    scales(0, b - 1)
                if b >= 2:
                    split(0, b - 2)
                    add_degrees(0, 2 * (b - 2))
                    add_degrees(0, 2 * (b - 2) + 1)
            fold_degrees(0)

            def chunk0(c, staged_base):
                for g in range(GROUPS):
                    check((c - 1) * GROUPS + g, g, staged_base + 16 * (g // STAGES + 1))
                    add_degrees(c, g)
                    if g == 3 and not (isinstance(c, int) and c == 1):
                        scales(1, c - 2)
                    if g == 12:
                        epilogue0(c - 1)
                fold_degrees(c)

            chunk0(1, 16 * GROUPS // STAGES)
            before = chain.count
            per_chunk = None
            with dve.Fori(2, KEPT_LAST + 1) as c:
                chain.base, chain.count = 0, 0
                per_chunk = STEPS0
                chain.base = c * per_chunk + (before - 2 * per_chunk)
                chunk0(c, c * (16 * GROUPS // STAGES))
                assert chain.count == per_chunk, chain.count
            chain.base, chain.count = 0, before + (KEPT_LAST - 1) * per_chunk
            for g in range(GROUPS):
                add_degrees(CHUNKS - 1, g)
                if g == 1:
                    scales(1, CHUNKS - 3)
                if g == 8:
                    epilogue0(CHUNKS - 2)
                if g == 9:
                    scales(1, CHUNKS - 2)
                if g in (11, 13, 15):
                    split(1, (g - 11) // 2)
            fold_degrees(CHUNKS - 1)

            def check1(c, g):
                n = load_index(1, c, g)
                check(CHECKS0 + n - ALL0, n % STAGES, 16 * (n // STAGES + 1))

            for b in range(3, CHUNKS - 1):
                split(1, b)
                check1(0, b - 3)
            epilogue0(CHUNKS - 1)
            scales(1, CHUNKS - 1)
            split(1, CHUNKS - 1)
            for g in range(4, GROUPS):
                check1(0, g)
            for g in range(8):
                check1(CHUNKS - 1, g)
            epilogue1(0)
            with dve.Fori(1, CHUNKS - 2) as c:
                epilogue1(c)
            for g in range(8, 12):
                check1(CHUNKS - 1, g)
            epilogue1(CHUNKS - 2)
            for g in range(12, GROUPS):
                check1(CHUNKS - 1, g)
            epilogue1(CHUNKS - 1)

        @block.gpsimd
        def _(pool):
            pool.memset(eye[:], 0.0).then_inc(consts, 1)
            pool.wait_ge(consts, 1)
            pool.affine_select(out=eye[:], in_=eye[:], compare_op=ALU.not_equal, fill=1.0, base=0,
                               pattern=[[-1, P]], channel_multiplier=1).then_inc(consts, 1)
            pool.memset(per_edge[:], 1.0 / BYTE_UNIT).then_inc(consts, 1)
            pool.wait_ge(bias_loaded, 16)
            for b in range(CHUNKS):
                rows = xs[:, b * BATCH:(b + 1) * BATCH, :]
                pool.wait_ge(h_ready, b + 1)
                pool.tensor_tensor(rows, rows, bias[:].unsqueeze(1).to_broadcast([P, BATCH, D]), ALU.add
                                   ).then_inc(biased, 1)

            diagonals = BATCH
            step = (CHUNK + P) // 4

            def add_eye(words, base):
                for j in range(diagonals):
                    o = base + j * step
                    d = words[:, o:o + P // 4] if isinstance(o, int) else words[:, bass.ds(o, P // 4)]
                    last = nc.gpsimd.tensor_tensor(d, d, eye32, ALU.add)
                last.then_inc(diag_added, 1)

            pool.wait_ge(diag_added, 1)
            pool.wait_ge(cast_done, ALL0 + 2)
            add_eye(ring32, 0)
            with pool.Fori(KEPT_FIRST, KEPT_LAST + 1) as c:
                tile_words = GROUP // 4
                add_eye(kept32, (c - KEPT_FIRST) * (GROUPS * tile_words) + c * (2 * tile_words))
            for b in range(CHUNKS - 1):
                pool.wait_ge(out_ready, b + 1)
                pool.dma_start(out[:, b * BATCH * D:(b + 1) * BATCH * D],
                               xs[:, b * BATCH:(b + 1) * BATCH, :].rearrange("p j d -> p (j d)")).then_inc(stored, 16)
            pool.wait_ge(cast_done, ALL0 + 2 * GROUPS)
            add_eye(ring32, (GROUPS - 2) % RING * (GROUP // 4))
            b = CHUNKS - 1
            pool.wait_ge(out_ready, b + 1)
            pool.dma_start(out[:, b * BATCH * D:(b + 1) * BATCH * D],
                           xs[:, b * BATCH:(b + 1) * BATCH, :].rearrange("p j d -> p (j d)")).then_inc(stored, 16)
            pool.wait_ge(stored, 16 * CHUNKS)


def kernel(x, adj, L0_gnn_W, L0_gnn_b, L1_gnn_W):
    import numpy as np
    import concourse.bacc as bacc
    from concourse.bass_utils import run_bass_kernel_spmd

    x, adj, w0, b0, w1 = (np.asarray(a) for a in (x, adj, L0_gnn_W, L0_gnn_b, L1_gnn_W))
    arrays = {
        "x_in": np.ascontiguousarray(x.reshape(BLOCKS, P, D).transpose(1, 0, 2)).reshape(P, BLOCKS * D),
        "adj_in": np.ascontiguousarray(adj.reshape(CHUNKS, CHUNK, BLOCKS, P).transpose(0, 3, 2, 1)
                                       ).reshape(CHUNKS, P, BLOCKS * CHUNK),
        "w0_in": np.ascontiguousarray(w0.transpose(1, 0, 2)).reshape(D, D),
        "w1_in": np.ascontiguousarray(w1),
        "b_in": np.ascontiguousarray(b0).reshape(D),
    }
    nc = bacc.Bacc("TRN2", target_bir_lowering=False, num_devices=1)
    ins = [nc.dram_tensor(k, v.shape, DT.float32, kind="ExternalInput").ap() for k, v in arrays.items()]
    out = nc.dram_tensor("out", (P, BLOCKS * D), DT.float32, kind="ExternalOutput").ap()
    build(nc, *ins, out)
    r = run_bass_kernel_spmd(nc, [arrays], core_ids=[0])
    return np.ascontiguousarray(r.results[0]["out"].reshape(P, BLOCKS, D).transpose(1, 0, 2)).reshape(N, D)
```

```python
from contextlib import ExitStack

import concourse.bass as bass
from concourse import mybir
from concourse.alu_op_type import AluOpType as ALU

DT = mybir.dt
ACT = mybir.ActivationFunctionType

P = 128
N = 4096
D = 256
BLOCKS = N // P
CHUNK = 512
CHUNKS = N // CHUNK
BATCH = CHUNK // P
GROUP_BLOCKS = 2
GROUP = GROUP_BLOCKS * CHUNK
GROUPS = BLOCKS // GROUP_BLOCKS
STAGES = 4
RING = 8
KEPT_FIRST, KEPT_LAST = 1, CHUNKS - 2
KEPT = KEPT_LAST - KEPT_FIRST + 1
ALL0 = CHUNKS * GROUPS
CHECKS0 = KEPT * GROUPS
H_SCALE = 2.0 ** 11
A_UNIT = 2.0 ** -14
S_UNSCALE = 1.0 / (H_SCALE * A_UNIT)
BANKS_OF = (0, 1, 2, 0, 1, 0, 1, 2)
EPS = 1e-5
BYTE_UNIT = 4.0
STEPS0 = (BATCH + 5) + 6 + 1


def position(c, g):
    return 2 * g + c if isinstance(c, int) and c < 2 else c * GROUPS + g


def ring_use(layer, c, g):
    return (2 * layer + (c != 0)) * GROUPS + g


def load_index(layer, c, g):
    if layer == 0:
        return position(c, g)
    return ALL0 + (c != 0) * GROUPS + g


class Chain:

    def __init__(self, engine, sem):
        self.engine, self.sem, self.base, self.count = engine, sem, 0, 0

    def step(self, instruction):
        instruction.then_inc(self.sem, 1)
        self.count += 1

    def settle(self):
        self.engine.wait_ge(self.sem, self.base + self.count)

    def link(self, instruction):
        self.step(instruction)
        self.settle()


def build(nc, x_in, adj_in, w0_in, w1_in, b_in, out):
    with ExitStack() as ctx:
        def sb(name, shape, dt):
            return ctx.enter_context(nc.sbuf_tensor(name, shape, dt))

        def sem(name):
            return ctx.enter_context(nc.semaphore(name))

        kept = sb("kept", [P, KEPT * GROUPS * GROUP], DT.float8e5)
        ring = sb("ring", [P, RING * GROUP], DT.float8e5)
        stage = sb("stage", [P, STAGES, GROUP], DT.float32)
        hsplit = sb("hsplit", [P, BLOCKS, 2, D], DT.float16)
        xs = sb("xs", [P, BLOCKS, D], DT.float32)
        w = sb("w", [P, 2, D], DT.float32)
        st = sb("st", [P, 2, CHUNK], DT.float32)
        bias = sb("bias", [P, D], DT.float32)
        hfull = sb("hfull", [P, 2, BATCH, D], DT.float32)
        bad_out = sb("bad_out", [P, GROUP], DT.uint8)
        bad = sb("bad", [P, ALL0], DT.float32)
        byte_sum = sb("byte_sum", [P, 2, GROUP // 2], DT.uint16)
        edge_sum = sb("edge_sum", [P, 2, CHUNK], DT.bfloat16)
        per_edge = sb("per_edge", [P, 1], DT.bfloat16)
        eye = sb("eye", [P, P], DT.float32)
        eye8 = sb("eye8", [P, P], DT.float8e5)
        bn = sb("bn", [P, BATCH, 6], DT.float32)
        mean_twice = sb("mean_twice", [P, 2, BATCH], DT.float32)
        mean_diff = sb("mean_diff", [P, BATCH], DT.float32)
        m2_sum = sb("m2_sum", [P, BATCH], DT.float32)
        radicand = sb("radicand", [P, 2, CHUNKS, 2 * BATCH], DT.float32)
        root = sb("root", [P, 2, CHUNKS, 2 * BATCH], DT.float32)
        inv = sb("inv", [P, 2, CHUNKS, 2 * BATCH], DT.float32)
        newton = sb("newton", [P, 2 * BATCH], DT.float32)
        norm_scale = sb("norm_scale", [P, 2, BLOCKS], DT.float32)
        norm_bias = sb("norm_bias", [P, 2, BLOCKS], DT.float32)

        ps_s = [[ctx.enter_context(nc.psum_tensor(f"ps_s{a}{q}", [P, CHUNK], DT.float32)) for q in range(2)]
                for a in range(3)]
        ps_w = [ctx.enter_context(nc.psum_tensor(f"ps_w{j}", [P, CHUNK], DT.float32)) for j in range(2)]
        ps_deg = ps_w[0][:, D:D + BATCH]

        kept16 = kept[:].bitcast(DT.uint16)
        kept32 = kept[:].bitcast(DT.uint32)
        ring16 = ring[:].bitcast(DT.uint16)
        ring32 = ring[:].bitcast(DT.uint32)
        eye32 = eye8[:].bitcast(DT.uint32)

        x_loaded = [sem(f"x_loaded{b}") for b in range(CHUNKS)]
        staged = [sem(f"staged{s}") for s in range(STAGES)]
        w_loaded = sem("w_loaded")
        bias_loaded = sem("bias_loaded")
        cast_done = sem("cast_done")
        check_done = sem("check_done")
        deg_added = sem("deg_added")
        edge_sums = sem("edge_sums")
        pe_groups = sem("pe_groups")
        s_evacuated = sem("s_evacuated")
        w_product = sem("w_product")
        w_read = sem("w_read")
        degrees_read = sem("degrees_read")
        radicand_ready = sem("radicand_ready")
        root_ready = sem("root_ready")
        norm_ready = sem("norm_ready")
        h_ready = sem("h_ready")
        high_ready = sem("high_ready")
        split_ready = sem("split_ready")
        biased = sem("biased")
        consts = sem("consts")
        diag_added = sem("diag_added")
        out_ready = sem("out_ready")
        stored = sem("stored")
        dve_step = sem("dve_step")

        block = ctx.enter_context(nc.Block())

        def tile8(c, g):
            if KEPT_FIRST <= c <= KEPT_LAST:
                o = ((c - KEPT_FIRST) * GROUPS + g) * GROUP
                return kept[:, o:o + GROUP]
            s = g % RING
            return ring[:, s * GROUP:(s + 1) * GROUP]

        @block.sync
        def _(sp):
            def load(c, g, n, casts, checks=None):
                s = n % STAGES
                if casts is not None:
                    sp.wait_ge(cast_done, casts)
                if checks is not None:
                    sp.nop(nofuse=True)
                    sp.wait_ge(check_done, checks)
                src = adj_in[c, :, g * GROUP:(g + 1) * GROUP] if isinstance(c, int) else \
                    adj_in[bass.ds(c, 1), :, g * GROUP:(g + 1) * GROUP].rearrange("a p f -> (a p) f")
                sp.dma_start(stage[:, s, :], src).then_inc(staged[s], 16)

            def load_x(b):
                sp.dma_start(xs[:, b * BATCH:(b + 1) * BATCH, :],
                             x_in[:, b * BATCH * D:(b + 1) * BATCH * D].rearrange("p (j d) -> p j d", d=D)
                             ).then_inc(x_loaded[b], 16)

            def load_w(w_in):
                sp.dma_start(w[:], w_in.rearrange("(q p) e -> p q e", p=P)).then_inc(w_loaded, 16)

            def free_of(n):
                before = n - STAGES
                return (None, None) if before < 0 else (before + 1, before // 2 + 1 if before % 2 else None)

            load_x(0)
            load_x(1)
            for n in range(2 * GROUPS):
                load(n % 2, n // 2, n, *free_of(n))
                if n % 4 == 1 and n // 4 + 2 < CHUNKS:
                    load_x(n // 4 + 2)
                if n == 3:
                    sp.dma_start(bias[:], b_in.partition_broadcast(P)).then_inc(bias_loaded, 16)
                if n == 15:
                    load_w(w0_in)
            for g in range(GROUPS):
                n = 2 * GROUPS + g
                load(2, g, n, *(free_of(n) if g < STAGES else (n - STAGES + 1, GROUPS + g - STAGES + 1)))
            with sp.Fori(3, KEPT_LAST + 1) as c:
                for g in range(GROUPS):
                    load(c, g, g, c * GROUPS + (g - STAGES + 1), (c - 1) * GROUPS + (g - STAGES + 1))
            for g in range(GROUPS):
                n = load_index(0, CHUNKS - 1, g)
                load(CHUNKS - 1, g, n, n - STAGES + 1, min(CHECKS0, CHECKS0 + g - STAGES + 1))
            for c in (0, CHUNKS - 1):
                for g in range(GROUPS):
                    n = load_index(1, c, g)
                    load(c, g, n, n - STAGES + 1, max(CHECKS0, CHECKS0 + n - ALL0 - STAGES + 1))
                    if c == 0 and g == 4:
                        sp.wait_ge(w_product, CHUNKS * BATCH)
                        load_w(w1_in)

        @block.tensor
        def _(pe):
            def w_products(layer, c, j):
                def degrees():
                    pe.wait_ge(edge_sums, c + 1)
                    for i in range(BATCH):
                        nc.tensor.matmul(ps_deg[:, i:i + 1], edge_sum[:, c % 2, i * P:(i + 1) * P], per_edge[:],
                                         start=True, stop=True)

                if j == 0:
                    pe.wait_ge(s_evacuated, layer * (2 * CHUNKS) + 2 * (c + 1))
                    pe.wait_ge(w_loaded, layer * 16 + 16)
                if j >= 2 or c > 0:
                    pe.wait_ge(w_read, layer * (CHUNKS * BATCH) + (c * BATCH + j - 1))
                if j == 2:
                    pe.wait_ge(degrees_read, c + 1)
                if j == 0 and isinstance(layer, int):
                    if layer == 0:
                        degrees()
                elif j == 0:
                    with pe.If(layer == 0):
                        degrees()
                for q in range(2):
                    last = nc.tensor.matmul(ps_w[j % 2][:, 0:D], st[:, q, j * P:(j + 1) * P], w[:, q, :],
                                            start=q == 0, stop=q == 1)
                last.then_inc(w_product, 1)

            def products(layer, c, g):
                if c == 0 and g % 2 == 0:
                    pe.wait_ge(split_ready, layer * CHUNKS + (g // 2 + 1))
                if g // 2 == c:
                    pe.wait_ge(diag_added, layer * (c + 1) + 1)
                pe.wait_ge(cast_done, position(c, g) + 1)
                if not KEPT_FIRST <= c <= KEPT_LAST:
                    again = load_index(1, c, g) - load_index(0, c, g)
                    pe.wait_ge(cast_done, layer * again + (position(c, g) + 1))
                pe.nop(nofuse=True)
                for i in range(GROUP_BLOCKS):
                    m = g * GROUP_BLOCKS + i
                    for q in range(2):
                        for part in range(2):
                            last = nc.tensor.matmul(
                                ps_s[BANKS_OF[c]][q][:], hsplit[:, m, part, q * P:(q + 1) * P],
                                tile8(c, g)[:, i * CHUNK:(i + 1) * CHUNK],
                                start=m == 0 and part == 0, stop=m == BLOCKS - 1 and part == 1)
                last.then_inc(pe_groups, 1)

            pe.wait_ge(consts, 3)
            with pe.Fori(0, 2) as layer:
                for g in range(GROUPS):
                    products(layer, 0, g)
                    products(layer, 1, g)
                    if g < BATCH:
                        with pe.If(layer == 1):
                            w_products(0, CHUNKS - 1, g)
                for c in range(2, CHUNKS):
                    for g in range(GROUPS):
                        products(layer, c, g)
                        if c == 2 and 1 <= g <= BATCH:
                            w_products(layer, 0, g - 1)
                        if c == 2 and 7 <= g < 7 + BATCH:
                            w_products(layer, 1, g - 7)
                        if c > 2 and g % 2 == 1 and g // 2 < BATCH:
                            w_products(layer, c - 1, g // 2)
            for j in range(BATCH):
                w_products(1, CHUNKS - 1, j)

        @block.scalar
        def _(act):
            act.wait_ge(consts, 2)
            act.activation(eye8[:], eye[:], ACT.Copy, scale=A_UNIT, saturate=False).then_inc(diag_added, 1)

            def cast(layer, c, g):
                n = load_index(layer, c, g)
                act.wait_ge(staged[n % STAGES], 16 * (n // STAGES + 1))
                if not KEPT_FIRST <= c <= KEPT_LAST:
                    u = ring_use(layer, c, g) - RING
                    if u >= 0:
                        ulayer, rest = divmod(u, 2 * GROUPS)
                        uc, ug = (CHUNKS - 1) * (rest // GROUPS), rest % GROUPS
                        act.wait_ge(pe_groups, ulayer * ALL0 + position(uc, ug) + 1)
                        act.wait_ge(deg_added, min(ALL0, ulayer * ALL0 + position(uc, ug) + 1))
                nc.scalar.activation(tile8(c, g), stage[:, n % STAGES, :], ACT.Copy, scale=A_UNIT,
                                     saturate=False).then_inc(cast_done, 1)

            def square_roots(layer, b):
                k = 4 if layer == 0 else 8
                act.wait_ge(radicand_ready, layer * CHUNKS + b + 1)
                nc.scalar.activation(root[:, layer, b, 0:k], radicand[:, layer, b, 0:k], ACT.Sqrt
                                     ).then_inc(root_ready, 1)

            def normalise(layer, b):
                act.wait_ge(norm_ready, layer * CHUNKS + b + 1)
                if layer * CHUNKS + b >= 2:
                    act.wait_ge(split_ready, layer * CHUNKS + b - 1)
                for j in range(BATCH):
                    m = b * BATCH + j
                    last = nc.scalar.activation(hfull[:, b % 2, j, :], xs[:, m, :], ACT.Relu,
                                                bias=norm_bias[:, layer, m:m + 1], scale=norm_scale[:, layer, m:m + 1])
                last.then_inc(h_ready, 1)
                if layer == 1:
                    act.wait_ge(pe_groups, (CHUNKS - 1) * GROUPS + 2 * b + 2)
                act.wait_ge(h_ready, layer * CHUNKS + b + 1)
                nc.scalar.activation(hsplit[:, b * BATCH:(b + 1) * BATCH, 0, :], hfull[:, b % 2], ACT.Copy
                                     ).then_inc(high_ready, 1)

            def evacuate(layer, c):
                k = layer * CHUNKS + c
                act.wait_ge(pe_groups, layer * ALL0 + position(c, GROUPS - 1) + 1)
                if k > 0:
                    act.wait_ge(w_product, BATCH * k)
                for q in range(2):
                    nc.scalar.activation(st[:, q, :], ps_s[BANKS_OF[c]][q][:], ACT.Copy, scale=S_UNSCALE
                                         ).then_inc(s_evacuated, 1)

            square_roots(0, 0)
            normalise(0, 0)
            square_roots(0, 1)
            for b in range(CHUNKS):
                for g in (2 * b, 2 * b + 1):
                    cast(0, 0, g)
                    cast(0, 1, g)
                if b + 2 < CHUNKS:
                    square_roots(0, b + 2)
                if b + 1 < CHUNKS:
                    normalise(0, b + 1)
            for g in range(GROUPS):
                cast(0, 2, g)
                if g == 0:
                    evacuate(0, 0)
                if g == 6:
                    evacuate(0, 1)
                if g == 8:
                    square_roots(1, 0)
                if g == 14:
                    square_roots(1, 1)
            for c in range(3, CHUNKS - 1):
                for g in range(GROUPS):
                    cast(0, c, g)
                    if g == 4:
                        evacuate(0, c - 1)
                    if g == 14:
                        square_roots(1, c - 1)
            for g in range(GROUPS):
                cast(0, CHUNKS - 1, g)
                if g == 4:
                    evacuate(0, CHUNKS - 2)
                if g == 13:
                    square_roots(1, CHUNKS - 2)
                if g in (10, 12, 14):
                    normalise(1, (g - 10) // 2)
            for g in range(STAGES):
                cast(1, 0, g)
                if g < 3:
                    normalise(1, 3 + g)
            evacuate(0, CHUNKS - 1)
            normalise(1, 6)
            cast(1, 0, STAGES)
            cast(1, 0, STAGES + 1)
            square_roots(1, CHUNKS - 1)
            normalise(1, 7)
            for g in range(STAGES + 2, GROUPS):
                cast(1, 0, g)
            for g in range(RING):
                cast(1, CHUNKS - 1, g)
            for c in range(CHUNKS - 1):
                evacuate(1, c)
            for g in range(RING, GROUPS):
                cast(1, CHUNKS - 1, g)
            evacuate(1, CHUNKS - 1)

        @block.vector
        def _(dve):
            chain = Chain(dve, dve_step)

            def statistics(layer, b):
                turn = b % 2 if layer == 0 else 0
                if layer == 0 and b > 0:
                    dve.wait_ge(radicand_ready, b)
                if layer == 0 and b > 1:
                    dve.wait_ge(norm_ready, b - 1)
                for j in range(BATCH):
                    chain.step(nc.vector.bn_stats(bn[:, j, :], block_of(xs, b * BATCH + j)))
                mean_even, m2_even, mean_odd, m2_odd = (bn[:, :, i] for i in (1, 2, 4, 5))
                chain.settle()
                chain.step(nc.vector.tensor_tensor(mean_twice[:, turn], mean_even, mean_odd, ALU.add))
                chain.step(nc.vector.tensor_tensor(mean_diff[:], mean_even, mean_odd, ALU.subtract))
                chain.step(nc.vector.tensor_tensor(m2_sum[:], m2_even, m2_odd, ALU.add))
                chain.settle()
                chain.step(nc.vector.scalar_tensor_tensor(out=mean_diff[:], in0=mean_diff[:], scalar=0.25,
                                                          in1=mean_diff[:], op0=ALU.mult, op1=ALU.mult))
                chain.step(nc.vector.tensor_scalar(m2_sum[:], m2_sum[:], 1.0 / D, EPS, ALU.mult, ALU.add))
                chain.settle()
                nc.vector.tensor_tensor(part_of(radicand, layer, b, 0, BATCH), m2_sum[:], mean_diff[:], ALU.add
                                        ).then_inc(radicand_ready, 1)

            def block_of(t, m):
                return t[:, m, :] if isinstance(m, int) else t[:, bass.ds(m, 1), :].rearrange("p a d -> p (a d)")

            def part_of(t, layer, b, lo, hi):
                v = t[:, layer]
                return v[:, b, lo:hi] if isinstance(b, int) else \
                    v[:, bass.ds(b, 1), lo:hi].rearrange("p a d -> p (a d)")

            def four_of(t, layer, b):
                v = t[:, layer, :]
                return v[:, b * BATCH:(b + 1) * BATCH] if isinstance(b, int) else v[:, bass.ds(b * BATCH, BATCH)]

            def scales(layer, b, between=()):
                between = list(between)

                def link(instruction):
                    chain.step(instruction)
                    if between:
                        between.pop(0)()
                    chain.settle()

                k = BATCH * (layer + 1)
                rad, iv = part_of(radicand, layer, b, 0, k), part_of(inv, layer, b, 0, k)
                nw = newton[:, 0:k]
                dve.wait_ge(root_ready, b + (layer * CHUNKS + 1))
                link(nc.vector.reciprocal(iv, part_of(root, layer, b, 0, k)))
                link(nc.vector.tensor_tensor(nw, iv, iv, ALU.mult))
                link(nc.vector.tensor_tensor(nw, nw, rad, ALU.mult))
                link(nc.vector.tensor_scalar(nw, nw, -0.5, 1.5, ALU.mult, ALU.add))
                link(nc.vector.tensor_tensor(iv, iv, nw, ALU.mult))
                if layer == 0:
                    link(nc.vector.tensor_scalar(four_of(norm_scale, 0, b), iv, H_SCALE, None, ALU.mult))
                else:
                    link(nc.vector.scalar_tensor_tensor(
                        out=four_of(norm_scale, 1, b), in0=part_of(inv, 1, b, 0, BATCH), scalar=H_SCALE,
                        in1=part_of(inv, 1, b, BATCH, 2 * BATCH), op0=ALU.mult, op1=ALU.mult))
                nc.vector.scalar_tensor_tensor(
                    out=four_of(norm_bias, layer, b), in0=mean_twice[:, b % 2 if layer == 0 else 0], scalar=-0.5,
                    in1=four_of(norm_scale, layer, b), op0=ALU.mult, op1=ALU.mult).then_inc(norm_ready, 1)
                for work in between:
                    work()

            def split(layer, b):
                dve.wait_ge(high_ready, layer * CHUNKS + b + 1)
                high, low = (hsplit[:, b * BATCH:(b + 1) * BATCH, i, :] for i in range(2))
                nc.vector.tensor_tensor(low, hfull[:, b % 2], high, ALU.subtract).then_inc(split_ready, 1)

            def check(index, n, staged_count):
                s = n % STAGES
                dve.wait_ge(staged[s], staged_count)
                if not (isinstance(index, int) and index == 0):
                    dve.wait_ge(check_done, index)
                column = bad[:, index:index + 1] if isinstance(index, int) else bad[:, bass.ds(index, 1)]
                nc.vector.scalar_tensor_tensor(out=bad_out[:], in0=stage[:, s, :], scalar=1.0, in1=stage[:, s, :],
                                               op0=ALU.is_equal, op1=ALU.not_equal, accum_out=column
                                               ).then_inc(check_done, 1)

            def add_degrees(c, g, turn):
                dve.wait_ge(cast_done, position(c, g) + 1)
                words = GROUP // 2
                if not isinstance(c, int):
                    tile = kept16[:, bass.ds(c * (GROUPS * words) + (g - GROUPS * KEPT_FIRST) * words, words)]
                elif KEPT_FIRST <= c <= KEPT_LAST:
                    tile = kept16[:, ((c - KEPT_FIRST) * GROUPS + g) * words:((c - KEPT_FIRST) * GROUPS + g + 1) * words]
                else:
                    tile = ring16[:, g % RING * words:(g % RING + 1) * words]
                total = byte_sum[:, turn]
                if g == 0:
                    if not (isinstance(c, int) and c < 2):
                        dve.wait_ge(edge_sums, c - 1)
                    nc.vector.tensor_copy(total, tile).then_inc(deg_added, 1)
                else:
                    dve.wait_ge(deg_added, position(c, g) - (isinstance(c, int) and c < 2))
                    nc.vector.tensor_tensor(total, total, tile, ALU.add).then_inc(deg_added, 1)

            def fold_degrees(c, turn):
                half = GROUP // 4
                low, high = byte_sum[:, turn, 0:half], byte_sum[:, turn, half:]
                dve.wait_ge(deg_added, position(c, GROUPS - 1) + 1)
                chain.link(nc.vector.tensor_tensor(low, low, high, ALU.add))
                nc.vector.tensor_copy(edge_sum[:, turn], low.bitcast(DT.uint8)).then_inc(edge_sums, 1)

            def epilogue0(c, j):
                dve.wait_ge(w_product, c * BATCH + (j + 1))
                if j == 0:
                    dve.wait_ge(biased, c + 1)
                    nc.vector.tensor_scalar(part_of(radicand, 1, c, BATCH, 2 * BATCH), ps_deg, 1.0, None, ALU.add
                                            ).then_inc(degrees_read, 1)
                rows = block_of(xs, c * BATCH + j)
                nc.vector.tensor_tensor(rows, ps_w[j % 2][:, 0:D], rows, ALU.add).then_inc(w_read, 1)
                if j == BATCH - 1:
                    dve.wait_ge(radicand_ready, c + CHUNKS)
                    dve.wait_ge(norm_ready, c + CHUNKS)
                    dve.wait_ge(w_read, c * BATCH + BATCH)
                    dve.nop(nofuse=True)
                    statistics(1, c)

            def epilogue1(c):
                if not (isinstance(c, int) and c == 0):
                    dve.wait_ge(out_ready, c)
                for j in range(BATCH):
                    dve.wait_ge(w_product, c * BATCH + (CHUNKS * BATCH + j + 1))
                    nc.vector.tensor_scalar(hfull[:, 0, j, :], ps_w[j % 2][:, 0:D], part_of(inv, 1, c, BATCH + j, BATCH + j + 1),
                                            0.0, ALU.mult, ALU.max).then_inc(w_read, 1)
                dve.wait_ge(w_read, c * BATCH + (CHUNKS * BATCH + BATCH))
                rows = xs[:, c * BATCH:(c + 1) * BATCH, :] if isinstance(c, int) else xs[:, bass.ds(c * BATCH, BATCH), :]
                nc.vector.tensor_tensor(rows, hfull[:, 0], rows, ALU.add).then_inc(out_ready, 1)

            for b in range(2):
                dve.wait_ge(x_loaded[b], 16)
                statistics(0, b)
                scales(0, b)
            for b in range(CHUNKS):
                split(0, b)
                work = []
                for g in (2 * b, 2 * b + 1):
                    n = position(1, g)
                    work.append(lambda g=g, n=n: check(g, n, 16 * (n // STAGES + 1)))
                    work.append(lambda g=g: add_degrees(0, g, 0))
                    work.append(lambda g=g: add_degrees(1, g, 1))
                work.pop(0)()
                if b + 2 < CHUNKS:
                    dve.wait_ge(x_loaded[b + 2], 16)
                    statistics(0, b + 2)
                    scales(0, b + 2, work)
                else:
                    for piece in work:
                        piece()
            fold_degrees(0, 0)
            fold_degrees(1, 1)

            def checked_chunk(c, turn, staged_base):
                for g in range(GROUPS):
                    check((c - 1) * GROUPS + g, g, staged_base + 16 * (g // STAGES + 1))
                    add_degrees(c, g, turn)
                    if isinstance(c, int) and c == 2:
                        if 2 <= g < 2 + BATCH:
                            epilogue0(0, g - 2)
                        if g == 7:
                            scales(1, 0)
                        if 9 <= g < 9 + BATCH:
                            epilogue0(1, g - 9)
                    else:
                        if g == 3:
                            scales(1, c - 2)
                        if g % 2 == 1 and 5 <= g < 5 + 2 * BATCH:
                            epilogue0(c - 1, (g - 5) // 2)
                fold_degrees(c, turn)

            checked_chunk(2, 0, 2 * 16 * GROUPS // STAGES)
            before = chain.count
            with dve.Fori(3, KEPT_LAST, 2) as c:
                chain.base, chain.count = (c - 3) * STEPS0 + before, 0
                checked_chunk(c, 1, c * (16 * GROUPS // STAGES))
                checked_chunk(c + 1, 0, (c + 1) * (16 * GROUPS // STAGES))
                assert chain.count == 2 * STEPS0, chain.count
            chain.base, chain.count = 0, before + (KEPT_LAST - 2) * STEPS0
            for g in range(GROUPS):
                add_degrees(CHUNKS - 1, g, 1)
                if g == 1:
                    scales(1, CHUNKS - 3)
                if g % 2 == 1 and 5 <= g < 5 + 2 * BATCH:
                    epilogue0(CHUNKS - 2, (g - 5) // 2)
                if g == 13:
                    scales(1, CHUNKS - 2)
                if g in (12, 14, 15):
                    split(1, (12, 14, 15).index(g))
            fold_degrees(CHUNKS - 1, 1)

            def check1(c, g):
                n = load_index(1, c, g)
                check(CHECKS0 + n - ALL0, n, 16 * (n // STAGES + 1))

            split(1, 3)
            check1(0, 0)
            split(1, 4)
            check1(0, 1)
            split(1, 5)
            check1(0, 2)
            epilogue0(CHUNKS - 1, 0)
            check1(0, 3)
            for j in range(1, BATCH):
                epilogue0(CHUNKS - 1, j)
                if j == 1:
                    split(1, 6)
            check1(0, STAGES)
            scales(1, CHUNKS - 1)
            split(1, 7)
            for g in range(STAGES + 1, GROUPS):
                check1(0, g)
            for g in range(8):
                check1(CHUNKS - 1, g)
            epilogue1(0)
            with dve.Fori(1, CHUNKS - 2) as c:
                epilogue1(c)
            for g in range(8, 12):
                check1(CHUNKS - 1, g)
            epilogue1(CHUNKS - 2)
            for g in range(12, GROUPS):
                check1(CHUNKS - 1, g)
            epilogue1(CHUNKS - 1)

        @block.gpsimd
        def _(pool):
            pool.memset(eye[:], 0.0).then_inc(consts, 1)
            pool.wait_ge(consts, 1)
            pool.affine_select(out=eye[:], in_=eye[:], compare_op=ALU.not_equal, fill=1.0, base=0,
                               pattern=[[-1, P]], channel_multiplier=1).then_inc(consts, 1)
            pool.memset(per_edge[:], 1.0 / BYTE_UNIT).then_inc(consts, 1)
            pool.wait_ge(bias_loaded, 16)
            for b in range(CHUNKS):
                rows = xs[:, b * BATCH:(b + 1) * BATCH, :]
                pool.wait_ge(h_ready, b + 1)
                pool.tensor_tensor(rows, rows, bias[:].unsqueeze(1).to_broadcast([P, BATCH, D]), ALU.add
                                   ).then_inc(biased, 1)

            diagonals = BATCH
            step = (CHUNK + P) // 4

            def add_eye(words, base):
                for j in range(diagonals):
                    o = base + j * step
                    d = words[:, o:o + P // 4] if isinstance(o, int) else words[:, bass.ds(o, P // 4)]
                    last = nc.gpsimd.tensor_tensor(d, d, eye32, ALU.add)
                last.then_inc(diag_added, 1)

            pool.wait_ge(diag_added, 1)
            pool.wait_ge(cast_done, ALL0 + 2)
            add_eye(ring32, 0)
            with pool.Fori(KEPT_FIRST, KEPT_LAST + 1) as c:
                tile_words = GROUP // 4
                add_eye(kept32, (c - KEPT_FIRST) * (GROUPS * tile_words) + c * (2 * tile_words))
            for b in range(CHUNKS - 1):
                pool.wait_ge(out_ready, b + 1)
                pool.dma_start(out[:, b * BATCH * D:(b + 1) * BATCH * D],
                               xs[:, b * BATCH:(b + 1) * BATCH, :].rearrange("p j d -> p (j d)")).then_inc(stored, 16)
            pool.wait_ge(cast_done, ALL0 + 2 * GROUPS)
            add_eye(ring32, (GROUPS - 2) % RING * (GROUP // 4))
            b = CHUNKS - 1
            pool.wait_ge(out_ready, b + 1)
            pool.dma_start(out[:, b * BATCH * D:(b + 1) * BATCH * D],
                           xs[:, b * BATCH:(b + 1) * BATCH, :].rearrange("p j d -> p (j d)")).then_inc(stored, 16)
            pool.wait_ge(stored, 16 * CHUNKS)


def kernel(x, adj, L0_gnn_W, L0_gnn_b, L1_gnn_W):
    import numpy as np
    import concourse.bacc as bacc
    from concourse.bass_utils import run_bass_kernel_spmd

    x, adj, w0, b0, w1 = (np.asarray(a) for a in (x, adj, L0_gnn_W, L0_gnn_b, L1_gnn_W))
    arrays = {
        "x_in": np.ascontiguousarray(x.reshape(BLOCKS, P, D).transpose(1, 0, 2)).reshape(P, BLOCKS * D),
        "adj_in": np.ascontiguousarray(adj.reshape(CHUNKS, CHUNK, BLOCKS, P).transpose(0, 3, 2, 1)
                                       ).reshape(CHUNKS, P, BLOCKS * CHUNK),
        "w0_in": np.ascontiguousarray(w0.transpose(1, 0, 2)).reshape(D, D),
        "w1_in": np.ascontiguousarray(w1),
        "b_in": np.ascontiguousarray(b0).reshape(D),
    }
    nc = bacc.Bacc("TRN2", target_bir_lowering=False, num_devices=1)
    ins = [nc.dram_tensor(k, v.shape, DT.float32, kind="ExternalInput").ap() for k, v in arrays.items()]
    out = nc.dram_tensor("out", (P, BLOCKS * D), DT.float32, kind="ExternalOutput").ap()
    build(nc, *ins, out)
    r = run_bass_kernel_spmd(nc, [arrays], core_ids=[0])
    return np.ascontiguousarray(r.results[0]["out"].reshape(P, BLOCKS, D).transpose(1, 0, 2)).reshape(N, D)
```

```python
from contextlib import ExitStack

import numpy as np

import concourse.bass as bass
from concourse import mybir
from concourse.alu_op_type import AluOpType as ALU

DT = mybir.dt
ACT = mybir.ActivationFunctionType

P = 128
N = 4096
D = 256
BLOCKS = N // P
CHUNK = 512
CHUNKS = N // CHUNK
BATCH = CHUNK // P
HALF = CHUNK // 2
GROUP_BLOCKS = 2
GROUP = GROUP_BLOCKS * CHUNK
GROUPS = BLOCKS // GROUP_BLOCKS
STAGES = 4
RING = 6
KEPT_FIRST, KEPT_LAST = 1, CHUNKS - 2
KEPT = KEPT_LAST - KEPT_FIRST + 1
ALL0 = CHUNKS * GROUPS
CHECKS0 = KEPT * GROUPS
H_SCALE = 2.0 ** 11
A_UNIT = 2.0 ** -14
S_UNSCALE = 1.0 / (H_SCALE * A_UNIT)
BANKS_OF = (0, 1, 2, 0, 2, 0, 1, 2)
EPS = 1e-5
HALVES, PE_BLOCKS, READS = (3, 7), (3, 3, 6, 6), (6, 6, 9, 9)
HALVES_EARLY, PE_EARLY, READS_EARLY = ((0, 4), (8, 11)), ((1, 1, 4, 4), (8, 8, 11, 11)), ((4, 4, 7, 7), (11, 11, 14, 14))
PE_TURN = (1, 1, 3, 3)
BYTE_UNIT = 4.0
GEN_FIRST = 1
GEN_ADDS = 2 * GROUPS + 1
STEPS0 = (BATCH + 5) + 6


def position(c, g):
    return 2 * g + c if isinstance(c, int) and c < 2 else c * GROUPS + g


def ring_last(layer, c, g):
    if g >= RING:
        return layer, c, g - RING
    if (layer, c) == (0, 0):
        return None
    before = (layer, 0) if c else (layer - 1, CHUNKS - 1)
    return *before, max(h for h in range(GROUPS) if h % RING == g)


def load_index(layer, c, g):
    if layer == 0:
        return position(c, g)
    return ALL0 + (c != 0) * GROUPS + g


class Chain:

    def __init__(self, engine, sem):
        self.engine, self.sem, self.base, self.count = engine, sem, 0, 0

    def step(self, instruction):
        instruction.then_inc(self.sem, 1)
        self.count += 1

    def settle(self):
        self.engine.wait_ge(self.sem, self.base + self.count)

    def link(self, instruction):
        self.step(instruction)
        self.settle()


def build(nc, x_in, adj_in, w0_in, w1_in, b_in, out):
    with ExitStack() as ctx:
        def sb(name, shape, dt):
            return ctx.enter_context(nc.sbuf_tensor(name, shape, dt))

        def sem(name):
            return ctx.enter_context(nc.semaphore(name))

        kept = sb("kept", [P, KEPT * GROUPS * GROUP], DT.float8e5)
        ring = sb("ring", [P, RING * GROUP], DT.float8e5)
        stage = sb("stage", [P, STAGES, GROUP], DT.float32)
        hsplit = sb("hsplit", [P, BLOCKS, 2, D], DT.float16)
        xs = sb("xs", [P, BLOCKS, D], DT.float32)
        w = sb("w", [P, 2, 2, D], DT.float32r)
        st = sb("st", [P, 2, 2, HALF], DT.float32r)
        bias = sb("bias", [P, D], DT.float32)
        hfull = sb("hfull", [P, 2, BATCH, D], DT.float32)
        bad_out = sb("bad_out", [P, GROUP], DT.uint8)
        bad = sb("bad", [P, ALL0], DT.float32)
        byte_sum = sb("byte_sum", [P, 2, GROUP // 2], DT.uint16)
        edge_sum = sb("edge_sum", [P, 2, CHUNK], DT.bfloat16)
        per_edge = sb("per_edge", [P, 1], DT.bfloat16)
        eye = sb("eye", [P, P], DT.float32)
        eye8 = sb("eye8", [P, P], DT.float8e5)
        bn = sb("bn", [P, BATCH, 6], DT.float32)
        mean_twice = sb("mean_twice", [P, 2, BATCH], DT.float32)
        mean_diff = sb("mean_diff", [P, BATCH], DT.float32)
        m2_sum = sb("m2_sum", [P, BATCH], DT.float32)
        radicand = sb("radicand", [P, 2, CHUNKS, 2 * BATCH], DT.float32)
        root = sb("root", [P, 2, CHUNKS, 2 * BATCH], DT.float32)
        inv = sb("inv", [P, 2, CHUNKS, 2 * BATCH], DT.float32)
        newton = sb("newton", [P, 2 * BATCH], DT.float32)
        norm_scale = sb("norm_scale", [P, 2, BLOCKS], DT.float32)
        norm_bias = sb("norm_bias", [P, 2, BLOCKS], DT.float32)

        bad_row = sb("bad_row", [P, 1], DT.float32)
        ones = sb("ones", [P, 1], DT.float32)
        flag = sb("flag", [1, 1], DT.int32)

        ps_s = [ctx.enter_context(nc.psum_tensor(f"ps_s{a}", [P, 2, CHUNK], DT.float32)) for a in range(3)]
        ps_w = [ctx.enter_context(nc.psum_tensor(f"ps_w{j}", [P, CHUNK], DT.float32)) for j in range(2)]
        ps_deg = ps_w[0][:, D:D + BATCH]

        gen_product_bank = [bank[:, 0:D] for bank in (ps_s[1][:, 0], ps_s[1][:, 1], ps_w[0], ps_w[1])]
        ps_gen_degrees = ps_s[2][:, 1, 0:BATCH]

        st32 = st[:].bitcast(DT.float32)
        w32 = w[:].bitcast(DT.float32)
        w_whole = edge_sum[:].rearrange("p a n -> p (a n)").bitcast(DT.float32).rearrange("p (q e) -> p q e", q=2)

        last_st = hfull[:, 1].rearrange("p a n -> p (a n)").rearrange("p (q n) -> p q n", q=2)

        kept16 = kept[:].bitcast(DT.uint16)
        kept32 = kept[:].bitcast(DT.uint32)
        ring16 = ring[:].bitcast(DT.uint16)
        ring32 = ring[:].bitcast(DT.uint32)
        eye32 = eye8[:].bitcast(DT.uint32)

        kept_f32 = kept[:].bitcast(DT.float32)
        taken = 0

        def take(*shape):
            nonlocal taken
            size = int(np.prod(shape))
            part = kept_f32[:, taken:taken + size]
            taken += size
            return part.rearrange("p (a b) -> p a b", b=shape[1]) if len(shape) == 2 else part

        gen_h = take(BLOCKS, D)
        gen_st = take(2, CHUNK)
        gen_w = take(2, D)
        gen_sums = take(CHUNK)
        gen_own = take(BATCH, D)
        gen_bn = take(BLOCKS, 6)
        gen_radicands, gen_root, gen_inv, gen_newton = (take(2 * BLOCKS) for _ in range(4))
        gen_mean_twice, gen_mean_diff, gen_m2_sum, gen_scale, gen_bias = (take(BLOCKS) for _ in range(5))

        x_loaded = [sem(f"x_loaded{b}") for b in range(CHUNKS)]
        staged = [sem(f"staged{s}") for s in range(STAGES)]
        w_loaded = sem("w_loaded")
        bias_loaded = sem("bias_loaded")
        cast_done = sem("cast_done")
        check_done = sem("check_done")
        deg_added0 = sem("deg_added0")
        deg_added = sem("deg_added")
        sums_halved = sem("sums_halved")
        edge_sums = sem("edge_sums")
        pe_groups = sem("pe_groups")
        w_high_ready = sem("w_high_ready")
        w_ready = sem("w_ready")
        st_high_ready = sem("st_high_ready")
        st_ready = sem("st_ready")
        last_st_ready = sem("last_st_ready")
        w_product = sem("w_product")
        w_read = sem("w_read")
        degrees_read = sem("degrees_read")
        radicand_ready = sem("radicand_ready")
        root_ready = sem("root_ready")
        norm_ready = sem("norm_ready")
        h_ready = sem("h_ready")
        high_ready = sem("high_ready")
        split_ready = sem("split_ready")
        half_h_ready = sem("half_h_ready")
        half_high_ready = sem("half_high_ready")
        half_split_ready = sem("half_split_ready")
        biased = sem("biased")
        consts = sem("consts")
        diag_added = sem("diag_added")
        out_ready = sem("out_ready")
        stored = sem("stored")
        last_stored = sem("last_stored")
        dve_step = sem("dve_step")
        bad_counted = sem("bad_counted")
        flag_summed = sem("flag_summed")
        flag_ready = sem("flag_ready")
        gen_x_loaded = sem("gen_x_loaded")
        gen_w_loaded = sem("gen_w_loaded")
        gen_tile = [sem(f"gen_tile{s}") for s in range(2)]
        gen_used = sem("gen_used")
        gen_added = sem("gen_added")
        gen_own_ready = sem("gen_own_ready")
        gen_radicand = sem("gen_radicand")
        gen_root_ready = sem("gen_root_ready")
        gen_h_ready = sem("gen_h_ready")
        gen_evacuated = sem("gen_evacuated")
        gen_product = sem("gen_product")
        gen_rows = sem("gen_rows")
        gen_stored = sem("gen_stored")
        gen_step = sem("gen_step")

        block = ctx.enter_context(nc.Block())

        def tile8(c, g):
            if KEPT_FIRST <= c <= KEPT_LAST:
                o = ((c - KEPT_FIRST) * GROUPS + g) * GROUP
                return kept[:, o:o + GROUP]
            s = g % RING
            return ring[:, s * GROUP:(s + 1) * GROUP]

        def any_bad(engine):
            engine.wait_ge(flag_ready, 1)
            return engine.value_load(flag[0:1, 0:1], min_val=0, max_val=N * N) > 0

        def bytes_of(c, g, kept_words, ring_words, words):
            if not isinstance(c, int):
                return kept_words[:, bass.ds(c * (GROUPS * words) + (g - GROUPS * KEPT_FIRST) * words, words)]
            if KEPT_FIRST <= c <= KEPT_LAST:
                o = ((c - KEPT_FIRST) * GROUPS + g) * words
                return kept_words[:, o:o + words]
            return ring_words[:, g % RING * words:(g % RING + 1) * words]

        def fold(engine, c, turn, low, high):
            if isinstance(c, int) and c == 0:
                engine.wait_ge(deg_added0, GROUPS)
            else:
                engine.wait_ge(deg_added, c * GROUPS)
            engine.tensor_tensor(low, low, high, ALU.add).then_inc(sums_halved, 1)
            engine.wait_ge(sums_halved, c + 1)
            if not (isinstance(c, int) and c < 2):
                engine.nop(nofuse=True)
                engine.wait_ge(degrees_read, c - 1)
                engine.nop(nofuse=True)
            engine.tensor_copy(edge_sum[:, turn], low.bitcast(DT.uint8)).then_inc(edge_sums, 1)

        @block.sync
        def _(sp):
            def load(c, g, n, casts, checks=None):
                s = n % STAGES
                if casts is not None:
                    sp.wait_ge(cast_done, casts)
                if checks is not None:
                    sp.nop(nofuse=True)
                    sp.wait_ge(check_done, checks)
                src = adj_in[c, :, g * GROUP:(g + 1) * GROUP] if isinstance(c, int) else \
                    adj_in[bass.ds(c, 1), :, g * GROUP:(g + 1) * GROUP].rearrange("a p f -> (a p) f")
                sp.dma_start(stage[:, s, :], src).then_inc(staged[s], 16)

            def load_x(b):
                sp.dma_start(xs[:, b * BATCH:(b + 1) * BATCH, :],
                             x_in[:, b * BATCH * D:(b + 1) * BATCH * D].rearrange("p (j d) -> p j d", d=D)
                             ).then_inc(x_loaded[b], 16)

            def load_w(w_in):
                sp.dma_start(w_whole, w_in.rearrange("(q p) e -> p q e", p=P)).then_inc(w_loaded, 16)

            def free_of(n):
                before = n - STAGES
                return (None, None) if before < 0 else (before + 1, before // 2 + 1 if before % 2 else None)

            load_x(0)
            load_x(1)
            for n in range(2 * GROUPS):
                load(n % 2, n // 2, n, *free_of(n))
                if n % 4 == 1 and n // 4 + 2 < CHUNKS:
                    load_x(n // 4 + 2)
                if n == 3:
                    sp.dma_start(bias[:], b_in.partition_broadcast(P)).then_inc(bias_loaded, 16)
                if n == 15:
                    load_w(w0_in)
            for g in range(GROUPS):
                n = 2 * GROUPS + g
                load(2, g, n, *(free_of(n) if g < STAGES else (n - STAGES + 1, GROUPS + g - STAGES + 1)))
            with sp.Fori(3, KEPT_LAST + 1) as c:
                for g in range(GROUPS):
                    load(c, g, g, c * GROUPS + (g - STAGES + 1), (c - 1) * GROUPS + (g - STAGES + 1))
            for g in range(GROUPS):
                n = load_index(0, CHUNKS - 1, g)
                load(CHUNKS - 1, g, n, n - STAGES + 1, min(CHECKS0, CHECKS0 + g - STAGES + 1))
            for c in (0, CHUNKS - 1):
                for g in range(GROUPS):
                    n = load_index(1, c, g)
                    load(c, g, n, n - STAGES + 1, max(CHECKS0, CHECKS0 + n - ALL0 - STAGES + 1))
                    if c == 0 and g == 6:
                        sp.wait_ge(w_product, CHUNKS * BATCH)
                        load_w(w1_in)

            for half in range(2):
                first = (CHUNKS - 1) * BATCH + half * BATCH // 2
                sp.wait_ge(out_ready, CHUNKS + half)
                sp.dma_start(out[:, first * D:(first + BATCH // 2) * D],
                             xs[:, first:first + BATCH // 2, :].rearrange("p j d -> p (j d)")).then_inc(last_stored, 16)
            sp.wait_ge(last_stored, 32)

            with sp.If(any_bad(sp)):
                sp.wait_ge(stored, 16 * (CHUNKS - 1))
                sp.dma_start(xs[:], x_in.rearrange("p (m d) -> p m d", d=D)).then_inc(gen_x_loaded, 16)
                sp.dma_start(gen_w, w0_in.rearrange("(q p) e -> p q e", p=P)).then_inc(gen_w_loaded, 16)
                for layer in range(2):
                    if layer == 1:
                        sp.wait_ge(gen_product, CHUNKS)
                        sp.dma_start(gen_w, w1_in.rearrange("(q p) e -> p q e", p=P)).then_inc(gen_w_loaded, 16)
                    with sp.Fori(0, CHUNKS) as c:
                        for g in range(GROUPS):
                            if g < 2:
                                sp.wait_ge(gen_rows, c + (layer * CHUNKS + GEN_FIRST))
                            else:
                                sp.wait_ge(gen_used, c * GROUPS + (layer * ALL0 + g - 1))
                                if layer == 0:
                                    sp.nop(nofuse=True)
                                    sp.wait_ge(gen_added, c * GEN_ADDS + (2 * g - 1))
                            sp.nop(nofuse=True)
                            sp.dma_start(stage[:, g % 2, :], adj_in[bass.ds(c, 1), :, g * GROUP:(g + 1) * GROUP]
                                         .rearrange("a p f -> (a p) f")).then_inc(gen_tile[g % 2], 16)

        @block.tensor
        def _(pe):
            def w_products(layer, c, j):
                def degrees():
                    pe.wait_ge(edge_sums, c + 1)
                    for i in range(BATCH):
                        nc.tensor.matmul(ps_deg[:, i:i + 1], edge_sum[:, c % 2, i * P:(i + 1) * P], per_edge[:],
                                         start=True, stop=True)

                if j == 0:
                    pe.wait_ge(w_ready, layer + 1)
                if j >= 2 or c > 0:
                    pe.wait_ge(w_read, layer * (CHUNKS * BATCH) + (c * BATCH + j - 1))
                if j == 0 and c > 0:
                    pe.wait_ge(degrees_read, c)
                if j == 2 and isinstance(layer, int):
                    if layer == 0:
                        degrees()
                elif j == 2:
                    with pe.If(layer == 0):
                        degrees()
                if j % 2 == 0:
                    pe.wait_ge(st_ready, layer * (2 * CHUNKS) + (2 * c + j // 2 + 1))
                n = j % 2 * P
                for q in range(2):
                    for a, b in ((0, 0), (0, 1), (1, 0)):
                        last = nc.tensor.matmul(ps_w[j % 2][:, 0:D], st[:, a, q, n:n + P], w[:, b, q, :],
                                                start=q == 0 and a == b, stop=q == 1 and a == 1)
                last.then_inc(w_product, 1)

            def products(layer, c, g):
                if c == 0 and g == 0:
                    pe.wait_ge(half_split_ready, 1)
                    with pe.If(layer == 1):
                        pe.wait_ge(split_ready, CHUNKS + 1)
                if c == 0 and (g == 1 or g > 0 and g % 2 == 0):
                    pe.wait_ge(split_ready, layer * CHUNKS + (g // 2 + 1))
                if g // 2 == c:
                    pe.wait_ge(diag_added, layer * (c + 1) + 1)
                pe.wait_ge(cast_done, position(c, g) + 1)
                if not KEPT_FIRST <= c <= KEPT_LAST:
                    again = load_index(1, c, g) - load_index(0, c, g)
                    pe.wait_ge(cast_done, layer * again + (position(c, g) + 1))
                pe.nop(nofuse=True)
                for i in range(GROUP_BLOCKS):
                    m = g * GROUP_BLOCKS + i
                    for q in range(2):
                        for part in range(2):
                            last = nc.tensor.matmul(
                                ps_s[BANKS_OF[c]][:, q, :], hsplit[:, m, part, q * P:(q + 1) * P],
                                tile8(c, g)[:, i * CHUNK:(i + 1) * CHUNK],
                                start=m == 0 and part == 0, stop=m == BLOCKS - 1 and part == 1)
                last.then_inc(pe_groups, 1)

            pe.wait_ge(consts, 4)
            with pe.Fori(0, 2) as layer:
                for g in range(GROUPS):
                    products(layer, 0, g)
                    products(layer, 1, g)
                    if g in PE_TURN:
                        with pe.If(layer == 1):
                            for j in range(BATCH):
                                if g == PE_TURN[j]:
                                    w_products(0, CHUNKS - 1, j)
                for c in range(2, CHUNKS):
                    for g in range(GROUPS):
                        products(layer, c, g)
                        for j in range(BATCH):
                            for before in range(2):
                                if c == 2 and g == PE_EARLY[before][j]:
                                    w_products(layer, before, j)
                            if c > 2 and g == PE_BLOCKS[j]:
                                w_products(layer, c - 1, j)
            pe.wait_ge(bad_counted, 1)
            nc.tensor.matmul(ps_s[BANKS_OF[0]][0:1, 0, 0:1], bad_row[:], ones[:], start=True, stop=True
                             ).then_inc(flag_summed, 1)
            for j in range(BATCH):
                pe.wait_ge(w_read, (2 * CHUNKS - 1) * BATCH + j - 1)
                for q in range(2):
                    if j == 0:
                        pe.wait_ge(last_st_ready, q + 1)
                    last = nc.tensor.matmul(ps_w[j % 2][:, 0:D], last_st[:, q, j * P:(j + 1) * P], w_whole[:, q, :],
                                            start=q == 0, stop=q == 1)
                last.then_inc(w_product, 1)

            with pe.If(any_bad(pe)):
                with pe.Fori(0, 2) as layer:
                    pe.wait_ge(gen_h_ready, layer + 1)
                    pe.nop(nofuse=True)
                    with pe.Fori(0, CHUNKS) as c:
                        pe.wait_ge(gen_evacuated, layer * (2 * CHUNKS) + c * 2 + GEN_FIRST)
                        for g in range(GROUPS):
                            pe.wait_ge(gen_tile[g % 2], layer * (ALL0 * 8) + c * (GROUPS * 8) + (g // 2 + 1) * 16)
                            for i in range(GROUP_BLOCKS):
                                m = g * GROUP_BLOCKS + i
                                for q in range(2):
                                    last = nc.tensor.matmul(ps_s[0][:, q, :], gen_h[:, m, q * P:(q + 1) * P],
                                                            stage[:, g % 2, i * CHUNK:(i + 1) * CHUNK],
                                                            start=m == 0, stop=m == BLOCKS - 1)
                            last.then_inc(gen_used, 1)
                            if g == 0:
                                pe.wait_ge(gen_own_ready, layer * CHUNKS + c + 1)
                                for j in range(BATCH):
                                    for q in range(2):
                                        nc.tensor.matmul(ps_s[0][:, q, j * P:(j + 1) * P],
                                                         gen_own[:, j, q * P:(q + 1) * P], eye[:],
                                                         start=False, stop=False)
                        pe.wait_ge(gen_evacuated, layer * (2 * CHUNKS) + c * 2 + (GEN_FIRST + 2))
                        pe.wait_ge(gen_w_loaded, layer * 16 + 16)
                        pe.wait_ge(gen_rows, layer * CHUNKS + c + GEN_FIRST)
                        with pe.If(layer == 0):
                            pe.wait_ge(gen_added, c * GEN_ADDS + GEN_ADDS)
                            for j in range(BATCH):
                                nc.tensor.matmul(ps_gen_degrees[:, j:j + 1], gen_sums[:, j * P:(j + 1) * P], ones[:],
                                                 start=True, stop=True)
                        for j in range(BATCH):
                            for q in range(2):
                                last = nc.tensor.matmul(gen_product_bank[j], gen_st[:, q, j * P:(j + 1) * P], gen_w[:, q, :],
                                                        start=q == 0, stop=q == 1)
                        last.then_inc(gen_product, 1)

        @block.scalar
        def _(act):
            act.wait_ge(consts, 2)
            act.activation(eye8[:], eye[:], ACT.Copy, scale=A_UNIT, saturate=False).then_inc(diag_added, 1)

            def cast(layer, c, g):
                n = load_index(layer, c, g)
                act.wait_ge(staged[n % STAGES], 16 * (n // STAGES + 1))
                if not KEPT_FIRST <= c <= KEPT_LAST:
                    last = ring_last(layer, c, g)
                    if last is not None:
                        ulayer, uc, ug = last
                        act.wait_ge(pe_groups, ulayer * ALL0 + position(uc, ug) + 1)
                        if ulayer == 0 and uc == 0:
                            act.wait_ge(deg_added0, ug + 1)
                        elif ulayer == 0:
                            act.wait_ge(deg_added, (uc - 1) * GROUPS + ug + 1)
                nc.scalar.activation(tile8(c, g), stage[:, n % STAGES, :], ACT.Abs, scale=A_UNIT,
                                     saturate=False).then_inc(cast_done, 1)

            def square_roots(layer, b):
                k = 4 if layer == 0 else 8
                act.wait_ge(radicand_ready, layer * CHUNKS + b + 1)
                nc.scalar.activation(root[:, layer, b, 0:k], radicand[:, layer, b, 0:k], ACT.Sqrt
                                     ).then_inc(root_ready, 1)

            def normalise(layer, b):
                act.wait_ge(norm_ready, layer * CHUNKS + b + 1)
                if layer * CHUNKS + b >= 2:
                    act.wait_ge(split_ready, layer * CHUNKS + b - 1)
                if layer == 0 and b == 0:
                    for half in range(2):
                        pair = slice(2 * half, 2 * half + 2)
                        for j in (2 * half, 2 * half + 1):
                            last = nc.scalar.activation(hfull[:, 0, j, :], xs[:, j, :], ACT.Relu,
                                                        bias=norm_bias[:, 0, j:j + 1], scale=norm_scale[:, 0, j:j + 1])
                        h_sem, high_sem = ((half_h_ready, half_high_ready), (h_ready, high_ready))[half]
                        last.then_inc(h_sem, 1)
                        act.wait_ge(h_sem, 1)
                        nc.scalar.activation(hsplit[:, pair, 0, :], hfull[:, 0, pair], ACT.Copy).then_inc(high_sem, 1)
                    return
                for j in range(BATCH):
                    m = b * BATCH + j
                    last = nc.scalar.activation(hfull[:, b % 2, j, :], xs[:, m, :], ACT.Relu,
                                                bias=norm_bias[:, layer, m:m + 1], scale=norm_scale[:, layer, m:m + 1])
                last.then_inc(h_ready, 1)
                if layer == 1:
                    act.wait_ge(pe_groups, (CHUNKS - 1) * GROUPS + 2 * b + 2)
                act.wait_ge(h_ready, layer * CHUNKS + b + 1)
                nc.scalar.activation(hsplit[:, b * BATCH:(b + 1) * BATCH, 0, :], hfull[:, b % 2], ACT.Copy
                                     ).then_inc(high_ready, 1)

            def split_w(layer):
                act.wait_ge(w_loaded, layer * 16 + 16)
                nc.scalar.activation(w[:, 0], w_whole, ACT.Copy).then_inc(w_high_ready, 1)

            def evacuate(layer, c, half):
                k = layer * CHUNKS + c
                act.wait_ge(pe_groups, layer * ALL0 + position(c, GROUPS - 1) + 1)
                if k > 0 or half > 0:
                    act.wait_ge(w_product, BATCH * k + 2 * half)
                nc.scalar.activation(st[:, 0], ps_s[BANKS_OF[c]][:, :, half * HALF:(half + 1) * HALF], ACT.Copy,
                                     scale=S_UNSCALE).then_inc(st_high_ready, 1)

            square_roots(0, 0)
            cast(0, 0, 0)
            normalise(0, 0)
            square_roots(0, 1)
            for b in range(CHUNKS):
                for g in (2 * b, 2 * b + 1):
                    if g > 0:
                        cast(0, 0, g)
                    cast(0, 1, g)
                if b == 0:
                    normalise(0, 1)
                if b + 2 < CHUNKS:
                    square_roots(0, b + 2)
                if 0 < b < CHUNKS - 1:
                    normalise(0, b + 1)
                if b == CHUNKS - 2:
                    split_w(0)
            for g in range(GROUPS):
                cast(0, 2, g)
                for before in range(2):
                    if g in HALVES_EARLY[before]:
                        evacuate(0, before, HALVES_EARLY[before].index(g))
                if g == 10:
                    square_roots(1, 0)
            for c in range(3, CHUNKS - 1):
                for g in range(GROUPS):
                    cast(0, c, g)
                    if c == 3 and g == 1:
                        square_roots(1, 1)
                    if g in HALVES:
                        evacuate(0, c - 1, HALVES.index(g))
                    if g == 14:
                        square_roots(1, c - 1)
            for g in range(GROUPS):
                cast(0, CHUNKS - 1, g)
                if g in HALVES:
                    evacuate(0, CHUNKS - 2, HALVES.index(g))
                if g == 13:
                    square_roots(1, CHUNKS - 2)
                if g in (10, 12, 14):
                    normalise(1, (g - 10) // 2)
            cast(1, 0, 0)
            cast(1, 0, 1)
            normalise(1, 3)
            normalise(1, 4)
            evacuate(0, CHUNKS - 1, 0)
            cast(1, 0, 2)
            normalise(1, 5)
            cast(1, 0, 3)
            evacuate(0, CHUNKS - 1, 1)
            cast(1, 0, 4)
            normalise(1, 6)
            cast(1, 0, 5)
            cast(1, 0, 6)
            square_roots(1, CHUNKS - 1)
            normalise(1, 7)
            for g in range(7, GROUPS):
                cast(1, 0, g)
            split_w(1)
            for g in range(RING):
                cast(1, CHUNKS - 1, g)
            for c in range(CHUNKS - 2):
                evacuate(1, c, 0)
                evacuate(1, c, 1)
            cast(1, CHUNKS - 1, RING)
            evacuate(1, CHUNKS - 2, 0)
            evacuate(1, CHUNKS - 2, 1)
            for g in range(RING + 1, GROUPS):
                cast(1, CHUNKS - 1, g)
            act.wait_ge(pe_groups, 2 * ALL0)
            for q in range(2):
                nc.scalar.activation(last_st[:, q, :], ps_s[BANKS_OF[CHUNKS - 1]][:, q, :], ACT.Copy, scale=S_UNSCALE
                                     ).then_inc(last_st_ready, 1)

            with act.If(any_bad(act)):
                act.wait_ge(stored, 16 * (CHUNKS - 1))
                act.wait_ge(last_stored, 32)
                act.nop(nofuse=True).then_inc(gen_evacuated, GEN_FIRST)
                for layer in range(2):
                    act.wait_ge(gen_radicand, layer + 1)
                    k = BLOCKS * (layer + 1)
                    nc.scalar.activation(gen_root[:, 0:k], gen_radicands[:, 0:k], ACT.Sqrt).then_inc(gen_root_ready, 1)
                    with act.Fori(0, CHUNKS) as c:
                        act.wait_ge(gen_used, c * GROUPS + (layer * ALL0 + GROUPS))
                        act.nop(nofuse=True)
                        if layer == 1:
                            act.wait_ge(gen_product, c + CHUNKS)
                        else:
                            with act.If(c > 0):
                                act.wait_ge(gen_product, c)
                                act.nop(nofuse=True)
                        for q in range(2):
                            nc.scalar.activation(gen_st[:, q, :], ps_s[0][:, q, :], ACT.Copy).then_inc(gen_evacuated, 1)

        @block.vector
        def _(dve):
            chain = Chain(dve, dve_step)

            def statistics(layer, b):
                turn = b % 2 if layer == 0 else 0
                if layer == 0 and b > 0:
                    dve.wait_ge(radicand_ready, b)
                if layer == 0 and b > 1:
                    dve.wait_ge(norm_ready, b - 1)
                for j in range(BATCH):
                    chain.step(nc.vector.bn_stats(bn[:, j, :], block_of(xs, b * BATCH + j)))
                mean_even, m2_even, mean_odd, m2_odd = (bn[:, :, i] for i in (1, 2, 4, 5))
                chain.settle()
                chain.step(nc.vector.tensor_tensor(mean_twice[:, turn], mean_even, mean_odd, ALU.add))
                chain.step(nc.vector.tensor_tensor(mean_diff[:], mean_even, mean_odd, ALU.subtract))
                chain.step(nc.vector.tensor_tensor(m2_sum[:], m2_even, m2_odd, ALU.add))
                chain.settle()
                chain.step(nc.vector.scalar_tensor_tensor(out=mean_diff[:], in0=mean_diff[:], scalar=0.25,
                                                          in1=mean_diff[:], op0=ALU.mult, op1=ALU.mult))
                chain.step(nc.vector.tensor_scalar(m2_sum[:], m2_sum[:], 1.0 / D, EPS, ALU.mult, ALU.add))
                chain.settle()
                nc.vector.tensor_tensor(part_of(radicand, layer, b, 0, BATCH), m2_sum[:], mean_diff[:], ALU.add
                                        ).then_inc(radicand_ready, 1)

            def block_of(t, m):
                return t[:, m, :] if isinstance(m, int) else t[:, bass.ds(m, 1), :].rearrange("p a d -> p (a d)")

            def part_of(t, layer, b, lo, hi):
                v = t[:, layer]
                return v[:, b, lo:hi] if isinstance(b, int) else \
                    v[:, bass.ds(b, 1), lo:hi].rearrange("p a d -> p (a d)")

            def four_of(t, layer, b):
                v = t[:, layer, :]
                return v[:, b * BATCH:(b + 1) * BATCH] if isinstance(b, int) else v[:, bass.ds(b * BATCH, BATCH)]

            def scales(layer, b, g=None):
                k = BATCH * (layer + 1)
                rad, iv = part_of(radicand, layer, b, 0, k), part_of(inv, layer, b, 0, k)
                nw = newton[:, 0:k]
                dve.wait_ge(root_ready, b + (layer * CHUNKS + 1))
                chain.step(nc.vector.reciprocal(iv, part_of(root, layer, b, 0, k)))
                if g is not None:
                    add_degrees0(g)
                chain.settle()
                chain.step(nc.vector.tensor_tensor(nw, iv, iv, ALU.mult))
                if g is not None:
                    check_early(g + 1)
                chain.settle()
                chain.step(nc.vector.tensor_tensor(nw, nw, rad, ALU.mult))
                if g is not None:
                    add_degrees0(g + 1)
                chain.settle()
                chain.link(nc.vector.tensor_scalar(nw, nw, -0.5, 1.5, ALU.mult, ALU.add))
                chain.link(nc.vector.tensor_tensor(iv, iv, nw, ALU.mult))
                if layer == 0:
                    chain.link(nc.vector.tensor_scalar(four_of(norm_scale, 0, b), iv, H_SCALE, None, ALU.mult))
                else:
                    chain.link(nc.vector.scalar_tensor_tensor(
                        out=four_of(norm_scale, 1, b), in0=part_of(inv, 1, b, 0, BATCH), scalar=H_SCALE,
                        in1=part_of(inv, 1, b, BATCH, 2 * BATCH), op0=ALU.mult, op1=ALU.mult))
                nc.vector.scalar_tensor_tensor(
                    out=four_of(norm_bias, layer, b), in0=mean_twice[:, b % 2 if layer == 0 else 0], scalar=-0.5,
                    in1=four_of(norm_scale, layer, b), op0=ALU.mult, op1=ALU.mult).then_inc(norm_ready, 1)

            def split(layer, b):
                if layer == 0 and b == 0:
                    for half, (high_sem, low_sem) in enumerate(((half_high_ready, half_split_ready),
                                                                (high_ready, split_ready))):
                        pair = slice(2 * half, 2 * half + 2)
                        dve.wait_ge(high_sem, 1)
                        nc.vector.tensor_tensor(hsplit[:, pair, 1, :], hfull[:, 0, pair], hsplit[:, pair, 0, :],
                                                ALU.subtract).then_inc(low_sem, 1)
                    return
                dve.wait_ge(high_ready, layer * CHUNKS + b + 1)
                high, low = (hsplit[:, b * BATCH:(b + 1) * BATCH, i, :] for i in range(2))
                nc.vector.tensor_tensor(low, hfull[:, b % 2], high, ALU.subtract).then_inc(split_ready, 1)

            def check(index, n, staged_count):
                s = n % STAGES
                dve.wait_ge(staged[s], staged_count)
                if not (isinstance(index, int) and index == 0):
                    dve.wait_ge(check_done, index)
                column = bad[:, index:index + 1] if isinstance(index, int) else bad[:, bass.ds(index, 1)]
                nc.vector.scalar_tensor_tensor(out=bad_out[:], in0=stage[:, s, :], scalar=1.0, in1=stage[:, s, :],
                                               op0=ALU.is_equal, op1=ALU.not_equal, accum_out=column
                                               ).then_inc(check_done, 1)

            def check_early(g):
                n = position(1, g)
                check(g, n, 16 * (n // STAGES + 1))

            def add_degrees0(g):
                dve.wait_ge(cast_done, position(0, g) + 1)
                tile, total = bytes_of(0, g, kept16, ring16, GROUP // 2), byte_sum[:, 0]
                if g == 0:
                    nc.vector.tensor_copy(total, tile).then_inc(deg_added0, 1)
                else:
                    dve.wait_ge(deg_added0, g)
                    nc.vector.tensor_tensor(total, total, tile, ALU.add).then_inc(deg_added0, 1)

            def split_w(layer):
                dve.wait_ge(w_high_ready, layer + 1)
                nc.vector.tensor_tensor(w[:, 1], w_whole, w32[:, 0], ALU.subtract).then_inc(w_ready, 1)

            def split_st(layer, c, pair, half):
                dve.wait_ge(st_high_ready, c * 2 + (layer * (2 * CHUNKS) + half + 1))
                nc.vector.scalar_tensor_tensor(out=st[:, 1], in0=ps_s[pair][:, :, half * HALF:(half + 1) * HALF],
                                               scalar=S_UNSCALE, in1=st32[:, 0], op0=ALU.mult, op1=ALU.subtract
                                               ).then_inc(st_ready, 1)

            def epilogue0(c, j):
                dve.wait_ge(w_product, c * BATCH + (j + 1))
                if j == 0:
                    dve.wait_ge(biased, c + 1)
                if j == 2:
                    nc.vector.tensor_scalar(part_of(radicand, 1, c, BATCH, 2 * BATCH), ps_deg, 1.0, None, ALU.add
                                            ).then_inc(degrees_read, 1)
                rows = block_of(xs, c * BATCH + j)
                nc.vector.tensor_tensor(rows, ps_w[j % 2][:, 0:D], rows, ALU.add).then_inc(w_read, 1)
                if j == BATCH - 1:
                    dve.wait_ge(radicand_ready, c + CHUNKS)
                    dve.wait_ge(norm_ready, c + CHUNKS)
                    dve.wait_ge(w_read, c * BATCH + BATCH)
                    dve.nop(nofuse=True)
                    statistics(1, c)

            def epilogue1(c, pair):
                if not (isinstance(c, int) and c == 0):
                    dve.wait_ge(out_ready, c)
                for j in range(BATCH):
                    if j % 2 == 0:
                        split_st(1, c, pair, j // 2)
                    dve.wait_ge(w_product, c * BATCH + (CHUNKS * BATCH + j + 1))
                    nc.vector.tensor_scalar(hfull[:, 0, j, :], ps_w[j % 2][:, 0:D], part_of(inv, 1, c, BATCH + j, BATCH + j + 1),
                                            0.0, ALU.mult, ALU.max).then_inc(w_read, 1)
                dve.wait_ge(w_read, c * BATCH + (CHUNKS * BATCH + BATCH))
                rows = xs[:, c * BATCH:(c + 1) * BATCH, :] if isinstance(c, int) else xs[:, bass.ds(c * BATCH, BATCH), :]
                nc.vector.tensor_tensor(rows, hfull[:, 0], rows, ALU.add).then_inc(out_ready, 1)

            def last_epilogue1():
                c, done = CHUNKS - 1, (2 * CHUNKS - 1) * BATCH
                dve.wait_ge(out_ready, c)
                for half in range(2):
                    for j in (2 * half, 2 * half + 1):
                        dve.wait_ge(w_product, done + j + 1)
                        nc.vector.tensor_scalar(hfull[:, 0, j, :], ps_w[j % 2][:, 0:D],
                                                part_of(inv, 1, c, BATCH + j, BATCH + j + 1), 0.0, ALU.mult, ALU.max
                                                ).then_inc(w_read, 1)
                        dve.wait_ge(w_read, done + j + 1)
                        rows = block_of(xs, c * BATCH + j)
                        last = nc.vector.tensor_tensor(rows, hfull[:, 0, j, :], rows, ALU.add)
                    last.then_inc(out_ready, 1)

            dve.wait_ge(x_loaded[0], 16)
            statistics(0, 0)
            scales(0, 0)
            dve.wait_ge(x_loaded[1], 16)
            statistics(0, 1)
            split(0, 0)
            scales(0, 1)
            for b in range(CHUNKS):
                check_early(2 * b)
                if b + 2 < CHUNKS:
                    dve.wait_ge(x_loaded[b + 2], 16)
                    statistics(0, b + 2)
                    scales(0, b + 2, 2 * b)
                else:
                    add_degrees0(2 * b)
                    check_early(2 * b + 1)
                    add_degrees0(2 * b + 1)
            split_w(0)
            dve.wait_ge(w_ready, 1)
            fold(nc.vector, 0, 0, byte_sum[:, 0, 0:GROUP // 4], byte_sum[:, 0, GROUP // 4:])

            def checked_chunk(c, turn, staged_base):
                for g in range(GROUPS):
                    check((c - 1) * GROUPS + g, g, staged_base + 16 * (g // STAGES + 1))
                    if isinstance(c, int) and c == 2:
                        for before in range(2):
                            if g in HALVES_EARLY[before]:
                                split_st(0, before, BANKS_OF[before], HALVES_EARLY[before].index(g))
                            for j in range(BATCH):
                                if g == READS_EARLY[before][j]:
                                    epilogue0(before, j)
                        if g == 12:
                            scales(1, 0)
                    else:
                        if g == 3:
                            scales(1, c - 2)
                        if g in HALVES:
                            split_st(0, c - 1, BANKS_OF[2 if turn else 3], HALVES.index(g))
                        for j in range(BATCH):
                            if g == READS[j]:
                                epilogue0(c - 1, j)

            checked_chunk(2, 0, 2 * 16 * GROUPS // STAGES)
            before = chain.count
            with dve.Fori(3, KEPT_LAST, 2) as c:
                chain.base, chain.count = (c - 3) * STEPS0 + before, 0
                checked_chunk(c, 1, c * (16 * GROUPS // STAGES))
                checked_chunk(c + 1, 0, (c + 1) * (16 * GROUPS // STAGES))
                assert chain.count == 2 * STEPS0, chain.count
            chain.base, chain.count = 0, before + (KEPT_LAST - 2) * STEPS0
            for g in range(GROUPS):
                if g == 1:
                    scales(1, CHUNKS - 3)
                if g in HALVES:
                    split_st(0, CHUNKS - 2, BANKS_OF[CHUNKS - 2], HALVES.index(g))
                for j in range(BATCH):
                    if g == READS[j]:
                        epilogue0(CHUNKS - 2, j)
                if g == 13:
                    scales(1, CHUNKS - 2)
                if g in (12, 14, 15):
                    split(1, (12, 14, 15).index(g))

            def check1(c, g):
                n = load_index(1, c, g)
                check(CHECKS0 + n - ALL0, n, 16 * (n // STAGES + 1))

            split(1, 3)
            check1(0, 0)
            split(1, 4)
            check1(0, 1)
            split_st(0, CHUNKS - 1, BANKS_OF[CHUNKS - 1], 0)
            check1(0, 2)
            split(1, 5)
            check1(0, 3)
            epilogue0(CHUNKS - 1, 0)
            epilogue0(CHUNKS - 1, 1)
            split_st(0, CHUNKS - 1, BANKS_OF[CHUNKS - 1], 1)
            check1(0, 4)
            split(1, 6)
            check1(0, 5)
            epilogue0(CHUNKS - 1, 2)
            epilogue0(CHUNKS - 1, 3)
            scales(1, CHUNKS - 1)
            check1(0, 6)
            split(1, 7)
            for g in range(7, GROUPS):
                check1(0, g)
            split_w(1)
            for g in range(4):
                check1(CHUNKS - 1, g)
            epilogue1(0, BANKS_OF[0])
            for g in range(4, 8):
                check1(CHUNKS - 1, g)
            epilogue1(1, BANKS_OF[1])
            with dve.Fori(2, CHUNKS - 3, 2) as c:
                epilogue1(c, BANKS_OF[2])
                epilogue1(c + 1, BANKS_OF[3])
            for g in range(8, 10):
                check1(CHUNKS - 1, g)
            epilogue1(CHUNKS - 2, BANKS_OF[CHUNKS - 2])
            for g in range(10, GROUPS):
                check1(CHUNKS - 1, g)
            dve.wait_ge(check_done, ALL0)
            nc.vector.tensor_reduce(bad_row[:], bad[:], mybir.AxisListType.X, ALU.add).then_inc(bad_counted, 1)
            dve.wait_ge(flag_summed, 1)
            nc.vector.tensor_copy(flag[:], ps_s[BANKS_OF[0]][0:1, 0, 0:1]).then_inc(flag_ready, 1)
            last_epilogue1()

            with dve.If(any_bad(dve)):
                steps = Chain(dve, gen_step)
                dve.wait_ge(stored, 16 * (CHUNKS - 1))
                dve.wait_ge(last_stored, 32)
                dve.nop(nofuse=True).then_inc(gen_rows, GEN_FIRST)
                nc.vector.memset(gen_radicands, 1.0).then_inc(gen_step, 1)
                steps.count += 1
                steps.settle()
                for layer in range(2):
                    if layer == 0:
                        dve.wait_ge(gen_x_loaded, 16)
                    else:
                        dve.wait_ge(gen_rows, CHUNKS + GEN_FIRST)
                    with dve.Fori(0, BLOCKS) as m:
                        nc.vector.bn_stats(gen_bn[:, bass.ds(m, 1), :].rearrange("p a d -> p (a d)"), block_of(xs, m)
                                           ).then_inc(gen_step, 1)
                    steps.count += BLOCKS
                    steps.settle()
                    mean_even, m2_even, mean_odd, m2_odd = (gen_bn[:, :, i] for i in (1, 2, 4, 5))
                    steps.step(nc.vector.tensor_tensor(gen_mean_twice, mean_even, mean_odd, ALU.add))
                    steps.step(nc.vector.tensor_tensor(gen_mean_diff, mean_even, mean_odd, ALU.subtract))
                    steps.link(nc.vector.tensor_tensor(gen_m2_sum, m2_even, m2_odd, ALU.add))
                    steps.step(nc.vector.scalar_tensor_tensor(out=gen_mean_diff, in0=gen_mean_diff, scalar=0.25,
                                                              in1=gen_mean_diff, op0=ALU.mult, op1=ALU.mult))
                    steps.link(nc.vector.tensor_scalar(gen_m2_sum, gen_m2_sum, 1.0 / D, EPS, ALU.mult, ALU.add))
                    nc.vector.tensor_tensor(gen_radicands[:, 0:BLOCKS], gen_m2_sum, gen_mean_diff, ALU.add
                                            ).then_inc(gen_radicand, 1)
                    dve.wait_ge(gen_root_ready, layer + 1)
                    k = BLOCKS * (layer + 1)
                    inverse, nw = gen_inv[:, 0:k], gen_newton[:, 0:k]
                    steps.link(nc.vector.reciprocal(inverse, gen_root[:, 0:k]))
                    steps.link(nc.vector.tensor_tensor(nw, inverse, inverse, ALU.mult))
                    steps.link(nc.vector.tensor_tensor(nw, nw, gen_radicands[:, 0:k], ALU.mult))
                    steps.link(nc.vector.tensor_scalar(nw, nw, -0.5, 1.5, ALU.mult, ALU.add))
                    steps.link(nc.vector.tensor_tensor(inverse, inverse, nw, ALU.mult))
                    if layer == 0:
                        scale = gen_inv[:, 0:BLOCKS]
                    else:
                        scale = gen_scale
                        steps.link(nc.vector.tensor_tensor(scale, gen_inv[:, 0:BLOCKS], gen_inv[:, BLOCKS:], ALU.mult))
                    steps.link(nc.vector.scalar_tensor_tensor(out=gen_bias, in0=gen_mean_twice, scalar=-0.5, in1=scale,
                                                              op0=ALU.mult, op1=ALU.mult))
                    with dve.Fori(0, BLOCKS) as m:
                        nc.vector.tensor_scalar(block_of(gen_h, m), block_of(xs, m), scale[:, bass.ds(m, 1)],
                                                gen_bias[:, bass.ds(m, 1)], ALU.mult, ALU.add).then_inc(gen_step, 1)
                    steps.count += BLOCKS
                    steps.settle()
                    nc.vector.tensor_scalar(gen_h[:], gen_h[:], 0.0, None, ALU.max).then_inc(gen_h_ready, 1)

                    dve.wait_ge(gen_h_ready, layer + 1)
                    with dve.Fori(0, CHUNKS) as c:
                        if layer == 1:
                            dve.wait_ge(gen_product, c + CHUNKS)
                        else:
                            with dve.If(c > 0):
                                dve.wait_ge(gen_product, c)
                                dve.nop(nofuse=True)
                        dve.nop(nofuse=True)
                        nc.vector.tensor_scalar(gen_own, gen_h[:, bass.ds(c * BATCH, BATCH), :], float(layer), None,
                                                ALU.mult).then_inc(gen_own_ready, 1)
                        if layer == 0:
                            nc.vector.memset(gen_sums, 0.0).then_inc(gen_added, 1)
                            for g in range(GROUPS):
                                dve.wait_ge(gen_tile[g % 2], c * (GROUPS * 8) + (g // 2 + 1) * 16)
                                for i in range(GROUP_BLOCKS):
                                    dve.wait_ge(gen_added, c * GEN_ADDS + (2 * g + i + 1))
                                    nc.vector.tensor_tensor(gen_sums, gen_sums, stage[:, g % 2, i * CHUNK:(i + 1) * CHUNK],
                                                            ALU.add).then_inc(gen_added, 1)
                        dve.wait_ge(gen_product, c + (layer * CHUNKS + 1))
                        rows = [block_of(xs, c * BATCH + j) for j in range(BATCH)]
                        if layer == 0:
                            nc.vector.tensor_scalar(gen_radicands[:, bass.ds(c * BATCH + BLOCKS, BATCH)], ps_gen_degrees,
                                                    1.0, None, ALU.add).then_inc(gen_step, 1)
                            for j in range(BATCH):
                                nc.vector.tensor_tensor(rows[j], rows[j], bias[:], ALU.add).then_inc(gen_step, 1)
                            dve.wait_ge(gen_step, c * (BATCH + 1) + (steps.count + BATCH + 1))
                            for j in range(BATCH):
                                last = nc.vector.tensor_tensor(rows[j], rows[j], gen_product_bank[j], ALU.add)
                        else:
                            dve.wait_ge(gen_rows, c + (CHUNKS + GEN_FIRST))
                            for j in range(BATCH):
                                nc.vector.tensor_scalar(hfull[:, 0, j, :], gen_product_bank[j],
                                                        gen_inv[:, bass.ds(c * BATCH + (BLOCKS + j), 1)], 0.0,
                                                        ALU.mult, ALU.max).then_inc(gen_step, 1)
                            dve.wait_ge(gen_step, c * BATCH + (steps.count + BATCH))
                            for j in range(BATCH):
                                last = nc.vector.tensor_tensor(rows[j], hfull[:, 0, j, :], rows[j], ALU.add)
                        last.then_inc(gen_rows, 1)
                    steps.count += CHUNKS * (BATCH + 1 - layer)

        @block.gpsimd
        def _(pool):
            pool.memset(eye[:], 0.0).then_inc(consts, 1)
            pool.wait_ge(consts, 1)
            pool.affine_select(out=eye[:], in_=eye[:], compare_op=ALU.not_equal, fill=1.0, base=0,
                               pattern=[[-1, P]], channel_multiplier=1).then_inc(consts, 1)
            pool.memset(per_edge[:], 1.0 / BYTE_UNIT).then_inc(consts, 1)
            pool.memset(ones[:], 1.0).then_inc(consts, 1)
            for b in range(1, CHUNKS):
                high, low = (hsplit[:, b * BATCH:(b + 1) * BATCH, i, :] for i in range(2))
                pool.wait_ge(high_ready, b + 1)
                pool.wait_ge(split_ready, b)
                pool.tensor_tensor(low, hfull[:, b % 2], high, ALU.subtract).then_inc(split_ready, 1)
            pool.wait_ge(bias_loaded, 16)

            def add_bias(b):
                rows = xs[:, b * BATCH:(b + 1) * BATCH, :]
                pool.wait_ge(h_ready, b + 1)
                pool.tensor_tensor(rows, rows, bias[:].unsqueeze(1).to_broadcast([P, BATCH, D]), ALU.add
                                   ).then_inc(biased, 1)

            sums32 = byte_sum[:].rearrange("p a n -> p (a n)").bitcast(DT.uint32).rearrange("p (a n) -> p a n", a=2)

            def add_degrees(c, g, turn):
                tile, total = bytes_of(c, g, kept32, ring32, GROUP // 4), sums32[:, turn]
                if g == 0:
                    return
                pool.wait_ge(cast_done, position(c, g) + 1)
                if g == 1:
                    first = bytes_of(c, 0, kept32, ring32, GROUP // 4)
                    pool.nop(nofuse=True)
                    pool.wait_ge(edge_sums, 1 if isinstance(c, int) and c == 1 else c - 1)
                    pool.tensor_tensor(total, first, tile, ALU.add).then_inc(deg_added, 2)
                else:
                    pool.nop(nofuse=True)
                    pool.wait_ge(deg_added, c * GROUPS + g - GROUPS)
                    pool.tensor_tensor(total, total, tile, ALU.add).then_inc(deg_added, 1)

            def fold_degrees(c, turn):
                fold(pool, c, turn, sums32[:, turn, 0:GROUP // 8], sums32[:, turn, GROUP // 8:])

            add_bias(0)
            add_bias(1)
            for g in range(GROUPS):
                add_degrees(1, g, 1)
            fold_degrees(1, 1)
            for g in range(GROUPS):
                add_degrees(2, g, 0)
                if g % 2 == 1 and g // 2 + 2 < CHUNKS:
                    add_bias(g // 2 + 2)
            fold_degrees(2, 0)
            with pool.Fori(3, KEPT_LAST, 2) as c:
                for i in range(2):
                    for g in range(GROUPS):
                        add_degrees(c + i, g, 1 - i)
                    fold_degrees(c + i, 1 - i)
            for g in range(GROUPS):
                add_degrees(CHUNKS - 1, g, 1)

            diagonals = BATCH
            step = (CHUNK + P) // 4

            def add_eye(words, base):
                for j in range(diagonals):
                    o = base + j * step
                    d = words[:, o:o + P // 4] if isinstance(o, int) else words[:, bass.ds(o, P // 4)]
                    last = nc.gpsimd.tensor_tensor(d, d, eye32, ALU.add)
                last.then_inc(diag_added, 1)

            pool.wait_ge(diag_added, 1)
            pool.wait_ge(cast_done, ALL0 + 2)
            add_eye(ring32, 0)
            fold_degrees(CHUNKS - 1, 1)
            with pool.Fori(KEPT_FIRST, KEPT_LAST + 1) as c:
                tile_words = GROUP // 4
                add_eye(kept32, (c - KEPT_FIRST) * (GROUPS * tile_words) + c * (2 * tile_words))
            for b in range(CHUNKS - 1):
                pool.wait_ge(out_ready, b + 1)
                pool.dma_start(out[:, b * BATCH * D:(b + 1) * BATCH * D],
                               xs[:, b * BATCH:(b + 1) * BATCH, :].rearrange("p j d -> p (j d)")).then_inc(stored, 16)
            pool.wait_ge(cast_done, ALL0 + 2 * GROUPS)
            add_eye(ring32, (GROUPS - 2) % RING * (GROUP // 4))
            pool.wait_ge(stored, 16 * (CHUNKS - 1))

            with pool.If(any_bad(pool)):
                pool.wait_ge(gen_rows, 2 * CHUNKS + GEN_FIRST)
                pool.dma_start(out.rearrange("p (m d) -> p m d", d=D), xs[:]).then_inc(gen_stored, 16)
                pool.wait_ge(gen_stored, 16)


def kernel(x, adj, L0_gnn_W, L0_gnn_b, L1_gnn_W):
    import concourse.bacc as bacc
    from concourse.bass_utils import run_bass_kernel_spmd

    x, adj, w0, b0, w1 = (np.asarray(a) for a in (x, adj, L0_gnn_W, L0_gnn_b, L1_gnn_W))
    arrays = {
        "x_in": np.ascontiguousarray(x.reshape(BLOCKS, P, D).transpose(1, 0, 2)).reshape(P, BLOCKS * D),
        "adj_in": np.ascontiguousarray(adj.reshape(CHUNKS, CHUNK, BLOCKS, P).transpose(0, 3, 2, 1)
                                       ).reshape(CHUNKS, P, BLOCKS * CHUNK),
        "w0_in": np.ascontiguousarray(w0.transpose(1, 0, 2)).reshape(D, D),
        "w1_in": np.ascontiguousarray(w1),
        "b_in": np.ascontiguousarray(b0).reshape(D),
    }
    nc = bacc.Bacc("TRN2", target_bir_lowering=False, num_devices=1)
    ins = [nc.dram_tensor(k, v.shape, DT.float32, kind="ExternalInput").ap() for k, v in arrays.items()]
    out = nc.dram_tensor("out", (P, BLOCKS * D), DT.float32, kind="ExternalOutput").ap()
    build(nc, *ins, out)
    r = run_bass_kernel_spmd(nc, [arrays], core_ids=[0])
    return np.ascontiguousarray(r.results[0]["out"].reshape(P, BLOCKS, D).transpose(1, 0, 2)).reshape(N, D)
```
